# Optimizing a Trainium2 kernel written in Bass

```python
import numpy as np
import jax
import jax.numpy as jnp

def _softmax(x, axis=-1):
    return jax.nn.softmax(x, axis=axis)

def _gelu(x):
    return jax.nn.gelu(x, approximate=True)

def _silu(x):
    return jax.nn.silu(x)

def _sigmoid(x):
    return jax.nn.sigmoid(x)

def _layernorm(x, axis=-1, eps=1e-05):
    m = jnp.mean(x, axis=axis, keepdims=True)
    v = jnp.var(x, axis=axis, keepdims=True)
    return (x - m) / jnp.sqrt(v + eps)

def _scatter_add(tgt, idx, src, axis=0):
    return tgt.at[idx].add(src)

def _segment_sum(src, seg, n):
    return jax.ops.segment_sum(src, seg, n)
kernel_name = 'mk_decoder_postln_d1_seqx_r8_7f679b'

def setup_inputs(seed: int=0):
    np.random.seed(seed)
    _w = jnp.asarray

    def _rec_inputs():
        import jax
        import jax.numpy as jnp
        _rk = jax.random.key(seed)
        x = -0.0002928 + 1 * jax.random.normal(jax.random.fold_in(_rk, 1), (16, 64, 256), jnp.float32)
        _lenS = 64 - jax.random.randint(jax.random.fold_in(_rk, 7), (16,), 0, max(1, 64 // 4) + 1, jnp.int32)
        _lenS2 = 64 - jax.random.randint(jax.random.fold_in(_rk, 8), (16,), 0, max(1, 64 // 4) + 1, jnp.int32)
        _ctx_2048P = jax.random.normal(jax.random.fold_in(_rk, 11), (16, 16, 256), jnp.float32)
        _ctx_2048c = jax.random.dirichlet(jax.random.fold_in(_rk, 511), 0.3 * jnp.ones((16,), jnp.float32), (16, 64))
        _ctx_2048t = jnp.einsum('bsk,bkd->bsd', _ctx_2048c, _ctx_2048P)
        _ctx_2048t = _ctx_2048t * jax.lax.rsqrt(jnp.mean(jnp.square(_ctx_2048t)) + 1e-12) * 0.953939
        ctx_2048 = -1.39393e-06 + 0.999914 * (_ctx_2048t + 0.3 * jax.random.normal(jax.random.fold_in(_rk, 611), (16, 64, 256), jnp.float32))
        return (x, ctx_2048)
    x, ctx_2048 = _rec_inputs()

    def _L0_attn_setup():
        import math
        import jax, jax.numpy as jnp
        import numpy as np
        HIDDEN = 256
        HEADS = 16
        HEAD_DIM = HIDDEN // HEADS
        key = jax.random.key(seed)
        kx, kq, kk, kv, ko = jax.random.split(key, 5)
        s = 1.0 / math.sqrt(HIDDEN)
        return {'x': jax.random.normal(kx, (2, 256, HIDDEN), dtype=jnp.float32), 'Wq': jax.random.normal(kq, (HIDDEN, HIDDEN), dtype=jnp.float32) * s, 'Wk': jax.random.normal(kk, (HIDDEN, HIDDEN), dtype=jnp.float32) * s, 'Wv': jax.random.normal(kv, (HIDDEN, HIDDEN), dtype=jnp.float32) * s, 'Wo': jax.random.normal(ko, (HIDDEN, HIDDEN), dtype=jnp.float32) * s}
    _L0_attn_all = _L0_attn_setup()
    _L0_attn_in = {k: v for k, v in _L0_attn_all.items() if k in ('Wq', 'Wk', 'Wv', 'Wo')}
    del _L0_attn_all

    def _L0_xattn_setup():
        import math
        import jax, jax.numpy as jnp
        import numpy as np
        N_HEADS = 8
        CHANNELS = 64
        K_CH = CHANNELS // N_HEADS
        THETA = 10000.0

        def _rope_freqs(length, dim):
            inv_freq = 1.0 / THETA ** (jnp.arange(0, dim, 2, dtype=jnp.float32) / dim)
            f = jnp.arange(length, dtype=jnp.float32)[:, None] * inv_freq[None, :]
            return jnp.concatenate([f, f], axis=-1)

        def _apply_rotary(pos, t):
            half = t.shape[-1] // 2
            rot = jnp.concatenate([-t[..., half:], t[..., :half]], axis=-1)
            return t * jnp.cos(pos) + rot * jnp.sin(pos)

        def _proj(inp, W, b):
            return jnp.einsum('oc,bct->bot', W, inp) + b[None, :, None]
        key = jax.random.key(seed)
        ks = jax.random.split(key, 10)
        B, C, T = (4, CHANNELS, 256)
        bound = math.sqrt(6.0 / (C + C))

        def w(k):
            return jax.random.uniform(k, (C, C), jnp.float32, -bound, bound)
        return {'x': jax.random.normal(ks[0], (B, C, T), jnp.float32), 'c': jax.random.normal(ks[1], (B, C, T), jnp.float32), 'Wq': w(ks[2]), 'bq': jnp.zeros((C,), jnp.float32), 'Wk': w(ks[3]), 'bk': jnp.zeros((C,), jnp.float32), 'Wv': w(ks[4]), 'bv': jnp.zeros((C,), jnp.float32), 'Wo': w(ks[5]), 'bo': jnp.zeros((C,), jnp.float32)}
    _L0_xattn_all = _L0_xattn_setup()
    _L0_xattn_in = {k: v for k, v in _L0_xattn_all.items() if k in ('Wq', 'bq', 'Wk', 'bk', 'Wv', 'bv', 'Wo', 'bo')}
    del _L0_xattn_all

    def _L0_ffn_setup():
        import jax, jax.numpy as jnp
        import numpy as np
        B, S, D = (4, 256, 256)
        E, F, K = (8, 128, 2)
        SF = 128
        EPS = 1e-06

        def _rmsnorm(x, w, eps=EPS):
            var = jnp.mean(x * x, axis=-1, keepdims=True)
            return x * jax.lax.rsqrt(var + eps) * w
        key = jax.random.key(seed)
        ks = jax.random.split(key, 9)
        g = lambda k, shape, scale: jax.random.normal(k, shape, jnp.float32) * scale
        return {'x': g(ks[0], (B, S, D), 1.0), 'rms_weight': jnp.ones((D,), jnp.float32), 'router_w': g(ks[1], (D, E), 0.02), 'w_gate': g(ks[2], (E, D, F), 0.02), 'w_up': g(ks[3], (E, D, F), 0.02), 'w_down': g(ks[4], (E, F, D), 0.02), 'sw_gate': g(ks[5], (D, SF), 0.02), 'sw_up': g(ks[6], (D, SF), 0.02), 'sw_down': g(ks[7], (SF, D), 0.02)}
    _L0_ffn_all = _L0_ffn_setup()
    _L0_ffn_in = {k: v for k, v in _L0_ffn_all.items() if k in ('rms_weight', 'router_w', 'w_gate', 'w_up', 'w_down', 'sw_gate', 'sw_up', 'sw_down')}
    del _L0_ffn_all
    return {'x': x, 'ctx_2048': ctx_2048, 'L0_attn_Wq': _L0_attn_in['Wq'], 'L0_attn_Wk': _L0_attn_in['Wk'], 'L0_attn_Wv': _L0_attn_in['Wv'], 'L0_attn_Wo': _L0_attn_in['Wo'], 'L0_xattn_Wq': _L0_xattn_in['Wq'], 'L0_xattn_bq': _L0_xattn_in['bq'], 'L0_xattn_Wk': _L0_xattn_in['Wk'], 'L0_xattn_bk': _L0_xattn_in['bk'], 'L0_xattn_Wv': _L0_xattn_in['Wv'], 'L0_xattn_bv': _L0_xattn_in['bv'], 'L0_xattn_Wo': _L0_xattn_in['Wo'], 'L0_xattn_bo': _L0_xattn_in['bo'], 'L0_ffn_rms_weight': _L0_ffn_in['rms_weight'], 'L0_ffn_router_w': _L0_ffn_in['router_w'], 'L0_ffn_w_gate': _L0_ffn_in['w_gate'], 'L0_ffn_w_up': _L0_ffn_in['w_up'], 'L0_ffn_w_down': _L0_ffn_in['w_down'], 'L0_ffn_sw_gate': _L0_ffn_in['sw_gate'], 'L0_ffn_sw_up': _L0_ffn_in['sw_up'], 'L0_ffn_sw_down': _L0_ffn_in['sw_down']}

def reference(x, ctx_2048, L0_attn_Wq, L0_attn_Wk, L0_attn_Wv, L0_attn_Wo, L0_xattn_Wq, L0_xattn_bq, L0_xattn_Wk, L0_xattn_bk, L0_xattn_Wv, L0_xattn_bv, L0_xattn_Wo, L0_xattn_bo, L0_ffn_rms_weight, L0_ffn_router_w, L0_ffn_w_gate, L0_ffn_w_up, L0_ffn_w_down, L0_ffn_sw_gate, L0_ffn_sw_up, L0_ffn_sw_down):
    import jax
    import jax.numpy as jnp

    def _L0_attn_ref(x, Wq, Wk, Wv, Wo):
        import math
        import jax, jax.numpy as jnp
        import numpy as np
        HIDDEN = 256
        HEADS = 16
        HEAD_DIM = HIDDEN // HEADS
        B, T, _ = x.shape
        q = x @ Wq.T
        k = x @ Wk.T
        v = x @ Wv.T
        q = q.reshape(B, T, HEADS, HEAD_DIM).transpose(0, 2, 1, 3)
        k = k.reshape(B, T, HEADS, HEAD_DIM).transpose(0, 2, 1, 3)
        v = v.reshape(B, T, HEADS, HEAD_DIM).transpose(0, 2, 1, 3)
        scale = 1.0 / math.sqrt(HEAD_DIM)
        attn = jnp.einsum('bhqd,bhkd->bhqk', q, k) * scale
        attn = jax.nn.softmax(attn, axis=-1)
        out = jnp.einsum('bhqk,bhkd->bhqd', attn, v)
        out = out.transpose(0, 2, 1, 3).reshape(B, T, HIDDEN)
        return out @ Wo.T

    def _L0_xattn_ref(x, c, Wq, bq, Wk, bk, Wv, bv, Wo, bo):
        import math
        import jax, jax.numpy as jnp
        import numpy as np
        N_HEADS = 8
        CHANNELS = 64
        K_CH = CHANNELS // N_HEADS
        THETA = 10000.0

        def _rope_freqs(length, dim):
            inv_freq = 1.0 / THETA ** (jnp.arange(0, dim, 2, dtype=jnp.float32) / dim)
            f = jnp.arange(length, dtype=jnp.float32)[:, None] * inv_freq[None, :]
            return jnp.concatenate([f, f], axis=-1)

        def _apply_rotary(pos, t):
            half = t.shape[-1] // 2
            rot = jnp.concatenate([-t[..., half:], t[..., :half]], axis=-1)
            return t * jnp.cos(pos) + rot * jnp.sin(pos)

        def _proj(inp, W, b):
            return jnp.einsum('oc,bct->bot', W, inp) + b[None, :, None]
        b, _, t_t = x.shape
        t_s = c.shape[2]
        q_emb = _rope_freqs(t_t, K_CH)
        k_emb = _rope_freqs(t_s, K_CH)

        def split_heads(t):
            return t.reshape(b, N_HEADS, K_CH, t.shape[2]).transpose(0, 1, 3, 2)
        q = split_heads(_proj(x, Wq, bq))
        k = split_heads(_proj(c, Wk, bk))
        v = split_heads(_proj(c, Wv, bv))
        q = _apply_rotary(q_emb, q)
        k = _apply_rotary(k_emb, k)
        scores = jnp.einsum('bhtc,bhsc->bhts', q, k) / math.sqrt(K_CH)
        p_attn = jax.nn.softmax(scores, axis=-1)
        out = jnp.einsum('bhts,bhsc->bhtc', p_attn, v)
        out = out.transpose(0, 1, 3, 2).reshape(b, N_HEADS * K_CH, t_t)
        return _proj(out, Wo, bo)

    def _L0_ffn_ref(x, rms_weight, router_w, w_gate, w_up, w_down, sw_gate, sw_up, sw_down):
        import jax, jax.numpy as jnp
        import numpy as np
        B, S, D = (4, 256, 256)
        E, F, K = (8, 128, 2)
        SF = 128
        EPS = 1e-06

        def _rmsnorm(x, w, eps=EPS):
            var = jnp.mean(x * x, axis=-1, keepdims=True)
            return x * jax.lax.rsqrt(var + eps) * w
        b, s, d = x.shape
        e = router_w.shape[1]
        h = _rmsnorm(x, rms_weight)
        ht = h.reshape(-1, d)
        t = ht.shape[0]
        logits = ht @ router_w
        probs = jax.nn.softmax(logits, axis=-1)
        topv, topi = jax.lax.top_k(probs, K)
        topv = topv / jnp.sum(topv, axis=-1, keepdims=True)
        w_dense = jnp.zeros((t, e), ht.dtype).at[jnp.arange(t)[:, None], topi].set(topv)
        g = jnp.einsum('td,edf->tef', ht, w_gate)
        u = jnp.einsum('td,edf->tef', ht, w_up)
        eo = jnp.einsum('tef,efd->ted', jax.nn.silu(g) * u, w_down)
        moe = jnp.einsum('te,ted->td', w_dense, eo)
        sh = jax.nn.silu(ht @ sw_gate) * (ht @ sw_up) @ sw_down
        return (moe + sh).reshape(b, s, d)
    x = _layernorm(x + _L0_attn_ref(x, L0_attn_Wq, L0_attn_Wk, L0_attn_Wv, L0_attn_Wo), axis=-1)
    x = _layernorm(x + _L0_xattn_ref(x, ctx_2048, L0_xattn_Wq, L0_xattn_bq, L0_xattn_Wk, L0_xattn_bk, L0_xattn_Wv, L0_xattn_bv, L0_xattn_Wo, L0_xattn_bo), axis=-1)
    x = _layernorm(x + _L0_ffn_ref(x, L0_ffn_rms_weight, L0_ffn_router_w, L0_ffn_w_gate, L0_ffn_w_up, L0_ffn_w_down, L0_ffn_sw_gate, L0_ffn_sw_up, L0_ffn_sw_down), axis=-1)
    return x

_drawn_inputs = setup_inputs


def setup_inputs(seed=0):
    import zlib

    import numpy as np

    out = dict(_drawn_inputs(seed))
    spreads = {'L0_xattn_bq': (0.0, 0.429),
     'L0_xattn_bk': (0.0, 0.768),
     'L0_xattn_bv': (0.0, 0.8),
     'L0_xattn_bo': (0.0, 0.8),
     'L0_ffn_rms_weight': (1.0, 0.6)}
    factors = {'L0_ffn_router_w': 7.084,
     'L0_ffn_w_gate': 6.242,
     'L0_ffn_w_up': 6.136,
     'L0_ffn_w_down': 6.151,
     'L0_ffn_sw_gate': 4.494,
     'L0_ffn_sw_up': 4.394,
     'L0_ffn_sw_down': 4.429}
    for name, (base, spread) in spreads.items():
        noise = np.random.default_rng([zlib.crc32(name.encode()), seed]).standard_normal(out[name].shape)
        drawn = base * np.exp(spread * noise) if base else spread * noise
        out[name] = jnp.asarray(drawn.astype(out[name].dtype))
    for name, factor in factors.items():
        out[name] = (out[name] * factor).astype(out[name].dtype)
    return out
```

```python
from contextlib import ExitStack

import numpy as np
import concourse.bass as bass
from concourse import mybir

F32 = mybir.dt.float32
F32R = mybir.dt.float32r
ALU = mybir.AluOpType
ACT = mybir.ActivationFunctionType
AX = mybir.AxisListType

P = 128
B, C, D = 16, 64, 256
NTOK = B * C
NPAIR = B // 2
H, HD = 16, 16
XH, XD = 8, 8
NE, F = 8, 128
LN_EPS, RMS_EPS = 1e-5, 1e-6
XROW = 32
MAXROW = 24
CREDIT = 32


def done(n):
    return n + 1 + CREDIT


def free(n, depth):
    return n + 1 + CREDIT - depth


def constant_block():
    p = np.arange(P)
    blocks = {}
    blocks["ident"] = np.eye(P)
    inv = (np.float32(1.0) / np.power(np.float32(10000.0), np.arange(0, XD, 2, dtype=np.float32) / np.float32(XD))).astype(np.float32)
    ang = (np.arange(D, dtype=np.float32)[:, None] * inv[None, :]).astype(np.float32)
    ang = np.concatenate([ang, ang], axis=1)
    blocks["cos"] = np.cos(ang).T[p % XD]
    blocks["sin"] = np.sin(ang).T[p % XD]
    blocks["signrow"] = np.broadcast_to(np.where(p % XD < XD // 2, -1.0, 1.0), (P, P))
    blocks["signcol"] = np.where(p % XD < XD // 2, -1.0, 1.0)[:, None]
    blocks["headmask"] = (p[:, None] // HD == np.arange(8)[None, :])
    blocks["fold"] = (p[:, None] % C == np.arange(C)[None, :])
    blocks["sameb"] = (p[:, None] // C == p[None, :] // C)
    blocks["onescol"] = (p % XROW == MAXROW)[:, None]
    blocks["before"] = np.broadcast_to((np.arange(NE)[None, :] < np.arange(NE)[:, None]).reshape(1, NE * NE), (P, NE * NE))
    sel = np.zeros((P, 2, 2, 2, 2, P))
    for w, parts in enumerate(((0, 0, 1), (0, 1, 0))):
        for b in range(2):
            for h in range(XH):
                for c, part in enumerate(parts):
                    for d in range(XD):
                        sel[64 * b + XD * h + d, w, b, h // 4, part, XROW * (h % 4) + XD * c + d] = 1
    blocks["sel"] = sel.reshape(P, -1)
    at, cols = {}, 0
    for k, v in blocks.items():
        at[k] = (cols, cols + v.shape[1])
        cols += v.shape[1]
    return np.concatenate([np.asarray(v, np.float32) for v in blocks.values()], axis=1), at


def build(nc, I, out):
    _, CAT = constant_block()
    ncon = max(v[1] for v in CAT.values())
    ctx = ExitStack()
    with ctx:
        def sb(name, shape, dt=F32):
            return ctx.enter_context(nc.sbuf_tensor("b_" + name, shape, dt))

        def sem(name):
            return ctx.enter_context(nc.semaphore(name))

        bank = ctx.enter_context(nc.psum_tensor("bank", [P, 8, 512], F32))
        con = sb("con", [P, ncon])
        K = lambda k: con[:, CAT[k][0]:CAT[k][1]]
        x_sb = sb("x", [P, NPAIR, D])
        xT = sb("xT", [P, 2, NTOK])
        wqkv = sb("wqkv", [P, 3, 2, D])
        wo = sb("wo", [P, 2, D])
        sel_r = sb("sel_r", [P, 16, P], F32R)
        sameb_r = sb("sameb_r", [P, P], F32R)
        cx = sb("cx", [P, NPAIR, D])
        xw = sb("xw", [P, 5, P])
        xwo = sb("xwo", [P, 2, C])
        xb = sb("xb", [P, 5])
        bvb = sb("bvb", [P, C])
        rmsw = sb("rmsw", [P, D])
        wgu = sb("wgu", [P, NE + 1, 2, 2, F])
        wdn = sb("wdn", [P, NE + 1, D])
        rw = sb("rw", [P, 2, NE])
        ysum = sb("ysum", [P, 2, D])
        stats = sb("stats", [P, 2, 6])
        mv = sb("mv", [P, 2, 2])
        rstd = sb("rstd", [P, 2])
        wait_here = sb("wait_here", [P, 1])
        half = sb("half", [P, 4])

        ld_x, ld_w, ld_xn, ld_c, ld_f = sem("ld_x"), sem("ld_w"), sem("ld_xn"), sem("ld_c"), sem("ld_f")
        ld_ctx = sem("ld_ctx")
        zeroed = sem("zeroed")
        vbd_zero = sem("vbd_zero")
        consts_ready = sem("consts_ready")
        p0_mm, p0_act, p0_dve = sem("p0_mm"), sem("p0_act"), sem("p0_dve")
        credit = {}

        def dsem(name):
            credit[name] = sem(name)
            return credit[name]

        dve_link, act_link, pool_link = sem("dve_link"), sem("act_link"), sem("pool_link")
        a_st, a_km, a_qm, a_vbd = dsem("a_st"), dsem("a_km"), dsem("a_qm"), dsem("a_vbd")
        a_s1, a_shift, a_s2, a_pt, a_pv = dsem("a_s1"), dsem("a_shift"), dsem("a_s2"), dsem("a_pt"), dsem("a_pv")
        a_on, a_t, a_ot, a_y = dsem("a_on"), dsem("a_t"), dsem("a_ot"), dsem("a_y")
        bn_done = dsem("bn_done")
        a_var, a_rstd, a_x1, a_sum = dsem("a_var"), dsem("a_rstd"), dsem("a_x1"), dsem("a_sum")
        x_pq, x_pk, x_ropes, x_roped, x_hi, x_lo, x_spread = (dsem("x_pq"), dsem("x_pk"), dsem("x_ropes"), dsem("x_roped"),
                                                     dsem("x_hi"), dsem("x_lo"), dsem("x_spread"))
        x_stack, x_cst, x_v, x_vst = dsem("x_stack"), dsem("x_cst"), dsem("x_v"), dsem("x_vst")
        x_km = [sem(f"x_km{s}") for s in range(4)]
        x_mrow = [sem(f"x_mrow{s}") for s in range(8)]
        x_s1, x_max, x_mt, x_mte = dsem("x_s1"), dsem("x_max"), dsem("x_mt"), dsem("x_mte")
        x_s2, x_exp, x_pv, x_norm = dsem("x_s2"), dsem("x_exp"), dsem("x_pv"), dsem("x_norm")
        x_y, x_ysum, x_var, x_rstd, x_x2 = dsem("x_y"), dsem("x_ysum"), dsem("x_var"), dsem("x_rstd"), dsem("x_x2")
        f_sq, f_ms, f_r, f_h, f_tp, f_hT = dsem("f_sq"), dsem("f_ms"), dsem("f_r"), dsem("f_h"), dsem("f_tp"), dsem("f_hT")
        f_lg, f_lsub, f_exp, f_w, f_wtp, f_wT, f_wrow, f_wb = (dsem("f_lg"), dsem("f_lsub"), dsem("f_exp"), dsem("f_w"),
                                                               dsem("f_wtp"), dsem("f_wT"), sem("f_wrow"), dsem("f_wb"))
        f_gu, f_silu, f_prod, f_act, f_dn = dsem("f_gu"), dsem("f_silu"), dsem("f_prod"), dsem("f_act"), dsem("f_dn")
        f_y, f_var, f_rstd, f_o, st_out = dsem("f_y"), dsem("f_var"), dsem("f_rstd"), dsem("f_o"), [sem("st_out0"), sem("st_out1")]
        credited = sem("credited")

        scopeA = ctx.enter_context(ExitStack())

        def sbA(name, shape, dt=F32):
            return scopeA.enter_context(nc.sbuf_tensor("a_" + name, shape, dt))

        QT = sbA("QT", [P, 2, NTOK])
        KT = sbA("KT", [P, 2, NTOK])
        V = sbA("V", [P, NPAIR, D])
        qst, kst = sbA("qst", [P, 2, 2, P]), sbA("kst", [P, 2, 2, P])
        qm, km = sbA("qm", [P, 2, 2, 8, P]), sbA("km", [P, 2, 2, 8, P])
        vbd = sbA("vbd", [P, 2, H, 2, HD + 1])
        negmax = sbA("negmax", [P, 2, H])
        shift = sbA("shift", [P, 2, H, C], F32R)
        pt = sbA("pt", [P, 2, H, C])
        rsum = sbA("rsum", [P, 2, 8, 2])
        on = sbA("on", [P, 2, 2, 8, HD])
        ot = sbA("ot", [P, 2, 2, 2, C])
        scopeA.close()
        scopeX = ctx.enter_context(ExitStack())

        def sbX(name, shape, dt=F32):
            return scopeX.enter_context(nc.sbuf_tensor("x_" + name, shape, dt))

        kmx = sbX("kmx", [P, 4, XH, D], F32R)
        qx = sbX("qx", [P, 4, 2, D], F32R)
        kstage = sbX("kstage", [P, 2, 2, D], F32R)
        rope = sbX("rope", [P, 2, 2, D])
        roped = sbX("roped", [P, 2, D])
        hilo = sbX("hilo", [P, 2, 2, 2, D], F32R)
        cst = sbX("cst", [P, D])
        vst = sbX("vst", [P, 2, 2, 2, XH, XROW])
        nmax = sbX("nmax", [P, 2, 2, 2, 4])
        mrow = sbX("mrow", [4, 2, 2, D], F32R)
        px = sbX("px", [P, 2, 4, 2, D])
        tn = sbX("tn", [P, 2, 16, 32])
        rs = sbX("rs", [P, 2, 16])
        onx = sbX("onx", [P, 4, 2, D])
        scopeX.close()
        scopeF = ctx.enter_context(ExitStack())

        def sbF(name, shape, dt=F32):
            return scopeF.enter_context(nc.sbuf_tensor("f_" + name, shape, dt))

        sq = sbF("sq", [P, D])
        ms = sbF("ms", [P, NPAIR])
        rr = sbF("rr", [P, NPAIR])
        hh = sbF("hh", [P, NPAIR, D])
        lg = sbF("lg", [P, NPAIR, NE])
        lmax = sbF("lmax", [P, NPAIR])
        ex = sbF("ex", [P, NPAIR, NE])
        gt = sbF("gt", [P, NPAIR, NE, NE])
        eq = sbF("eq", [P, NPAIR, NE, NE])
        rank = sbF("rank", [P, NPAIR, NE])
        wsel = sbF("wsel", [P, NPAIR, NE])
        wsum = sbF("wsum", [P, NPAIR])
        wT = sbF("wT", [NE, NTOK])
        wrow = sbF("wrow", [1, NE, NTOK])
        wb = sbF("wb", [P, 2, NTOK])
        sl = sbF("sl", [P, 2, 512])
        pr = sbF("pr", [P, 2, 512])
        act = sbF("act", [P, 2, 512])
        fy = sbF("fy", [P, 2, D])
        fo = sbF("fo", [P, 2, D])
        fpow = sbF("fpow", [P, NPAIR])
        scopeF.close()

        hT = xT

        class Chain:

            def __init__(self, eng, s):
                self.eng, self.s, self.base, self.k = eng, s, 0, 0

            def __call__(self, ins):
                self.k += 1
                ins.then_inc(self.s, 1)
                self.eng.wait_ge(self.s, self.base + self.k)

            def loop(self, it, first, per):
                self.start = self.base
                self.base = self.start + self.k_before + (it - first) * per
                self.k = 0

        def looped(eng, chain, lo, hi, body):
            start = chain.base + chain.k
            per = [0]

            with eng.Fori(lo, hi) as i:
                chain.k, per_guess = 0, body.links
                chain.base = start + (i - lo) * per_guess if per_guess else start
                body(i)
                assert chain.k == per_guess, (chain.k, per_guess)
            chain.base, chain.k = start + (hi - lo) * per_guess, 0

        cur = {}

        def valid(k, m, off):
            return (not isinstance(m, int)) or 0 <= m + off < B

        def x_steps(eng, chain, step):
            for k in range(-3, 4):
                step(k, k)
            lo, hi = 1, B // 4 - 1
            start = chain.base + chain.k if chain else 0
            with eng.Fori(lo, hi) as j:
                cur["half"] = 2 * j
                if chain:
                    chain.base, chain.k = start + (j - lo) * step.links, 0
                for k in range(4):
                    step(4 * j + k, k)
                if chain:
                    assert chain.k == step.links, chain.k
            if chain:
                chain.base, chain.k = start + (hi - lo) * step.links, 0
            for m in range(4 * hi, B + 1):
                step(m, m)

        def pair_of(m, k, off):
            if isinstance(m, int):
                return (m + off) // 2
            return cur["half"] + (k + off) // 2

        def valid_pair(m, k, off):
            return (not isinstance(m, int)) or 0 <= m + off < B

        def wait_km_staged(eng, m, k):
            if isinstance(m, int):
                if m >= 0:
                    eng.wait_ge(x_km[k % 4], 64 * (m // 4 + 1))
            else:
                eng.wait_ge(x_km[k % 4], ((m - k) * 16) + 64)

        def wait_mrow_free(eng, m, k, gr):
            s = ((k - 2) % 4) * 2 + gr
            if isinstance(m, int):
                if m >= 2:
                    eng.wait_ge(x_mrow[s], 16 * ((m - 2) // 4 + 1))
            else:
                eng.wait_ge(x_mrow[s], (m - k) * 4 + 16 * ((k - 2) // 4 + 1))

        def evac_phase0(eng, copy, s, parity):
            for n in range(parity, 12, 2):
                eng.wait_ge(p0_mm, n + 1)
                if n < 8:
                    w, gr, hf = n // 4, (n // 2) % 2, n % 2
                    ins = copy((QT, KT)[w][:, gr, 512 * hf:512 * hf + 512], bank[:, n, :])
                else:
                    v = n - 8
                    ins = copy(V[:, 2 * v:2 * v + 2, :].rearrange("p a d -> p (a d)"), bank[:, n % 8, :])
                ins.then_inc(s, 1)

        def order(i):
            return (NE if i < 2 else i // 2 - 1), i % 2

        def pair_floor(m, k):
            return m // 2 if isinstance(m, int) else cur["half"] + k // 2

        def pair_floor2(m, k):
            return (m + 2) // 2 if isinstance(m, int) else cur["half"] + (k + 2) // 2

        def wait_km(eng, m, k):
            if isinstance(m, int):
                eng.wait_ge(x_km[k % 4], 64 * (m // 4 + 1))
            else:
                eng.wait_ge(x_km[k % 4], (m - k) * 16 + 64 * (k // 4 + 1))

        def wait_mrow(eng, m, k, gr):
            s = (k % 4) * 2 + gr
            if isinstance(m, int):
                eng.wait_ge(x_mrow[s], 16 * (m // 4 + 1))
            else:
                eng.wait_ge(x_mrow[s], (m - k) * 4 + 16 * (k // 4 + 1))

        def free_bank2(eng, m, k, gr):
            if gr == 1:
                eng.wait_ge(x_mte, done(2 * m))
            else:
                km1 = k - 1
                if isinstance(m, int):
                    if m >= 1:
                        eng.wait_ge(x_mte, done(2 * m - 1))
                    if km1 % 2:
                        eng.wait_ge(x_vst, done(m // 2))
                    if km1 % 2 == 0 and m - 1 - 2 >= 0:
                        eng.wait_ge(x_ysum, done((m - 3) // 2))
                else:
                    eng.wait_ge(x_mte, done(2 * m - 1))
                    if km1 % 2:
                        eng.wait_ge(x_vst, done(cur["half"] + (km1 + 1) // 2))
                    else:
                        eng.wait_ge(x_ysum, done(cur["half"] + (km1 - 2) // 2))

        def free_bank2_v(eng, m, k):
            if isinstance(m, int):
                if 0 <= m < B:
                    eng.wait_ge(x_mte, done(2 * m + 1))
            else:
                eng.wait_ge(x_mte, done(2 * m + 1))


        block = ctx.enter_context(nc.Block())

        @block.sync
        def _(sp):
            sp.dma_start(xT[:, :, 0:512], I["xT"].rearrange("(c p) t -> p c t", p=P)[:, :, 0:512]).then_inc(ld_x, 16)
            sp.dma_start(wqkv[:], I["wqkv"]).then_inc(ld_w, 16)
            sp.dma_start(xT[:, :, 512:1024], I["xT"].rearrange("(c p) t -> p c t", p=P)[:, :, 512:1024]).then_inc(ld_x, 16)
            sp.dma_start(con[:, :], I["con"]).then_inc(ld_c, 16)
            sp.dma_start(wo[:], I["wo"]).then_inc(ld_xn, 16)
            sp.dma_start(x_sb[:], I["x"].rearrange("(n p) d -> p n d", p=P)).then_inc(ld_xn, 16)
            sp.dma_start(cx[:], I["ctx"].rearrange("(n p) d -> p n d", p=P)).then_inc(ld_ctx, 16)
            for o, name in ((xw, "xw"), (xwo, "xwo"), (xb, "xb")):
                sp.dma_start(o[:], I[name]).then_inc(ld_ctx, 16)
            sp.dma_start(bvb[:], I["xbv"].rearrange("(o n) -> o n", o=1).to_broadcast((P, C))).then_inc(ld_ctx, 16)
            sp.dma_start(rmsw[:], I["rms"].rearrange("(o n) -> o n", o=1).to_broadcast((P, D))).then_inc(ld_f, 16)
            for o, name in ((wgu, "wgu"), (wdn, "wdn"), (rw, "rw")):
                sp.dma_start(o[:], I[name]).then_inc(ld_f, 16)

            def x_step(m, k):
                if valid(k, m, 0):
                    sp.wait_ge(x_mte, done(2 * m + 1))
                    dst = qx[MAXROW:MAXROW + 3 * XROW + 1:XROW, k % 4, 1, :].bitcast(F32)
                    sp.dma_start(dst, mrow[:, k % 2, 1, :].bitcast(F32)).then_inc(x_mrow[(k % 4) * 2 + 1], 16)
                if valid(k, m, 2):
                    sp.wait_ge(x_stack, done(2 * (m + 2) + 1))
                    sp.wait_ge(x_s2, free(8 * (m + 2) + 7, 32))
                    for j in range(4):
                        r = slice(XROW * j, XROW * j + XROW)
                        sp.dma_start(kmx[r, (k + 2) % 4, j::4, :].bitcast(F32),
                                     kstage[r, k % 2, :, :].bitcast(F32)).then_inc(x_km[(k + 2) % 4], 16)
                if valid(k, m, 1):
                    sp.wait_ge(x_mte, done(2 * (m + 1)))
                    dst = qx[MAXROW:MAXROW + 3 * XROW + 1:XROW, (k + 1) % 4, 0, :].bitcast(F32)
                    sp.dma_start(dst, mrow[:, (k + 1) % 2, 0, :].bitcast(F32)).then_inc(x_mrow[((k + 1) % 4) * 2], 16)

            x_steps(sp, None, x_step)

            sp.wait_ge(f_wT, done(0))
            sp.dma_start(wrow[:], wT[:]).then_inc(f_wrow, 16)
            for t in range(NPAIR):
                sp.wait_ge(f_o, done(t))
                sp.dma_start(out.rearrange("(n p) d -> p n d", p=P)[:, t, :], fo[:, t % 2, :]).then_inc(st_out[t % 2], 16)
            for s in st_out:
                sp.wait_ge(s, 16 * (NPAIR // 2))

        @block.gpsimd
        def _(pool):
            g = nc.gpsimd
            link = Chain(pool, pool_link)
            for s in credit.values():
                pool.sem_inc(s, CREDIT)
            pool.sem_inc(credited, 1)
            g.memset(half[:, 0:1], -0.5)
            g.memset(half[:, 1:2], LN_EPS)
            g.memset(half[:, 2:3], RMS_EPS)
            pool.wait_ge(ld_c, 16)
            pool.wait_ge(p0_act, 6)
            pool.wait_ge(p0_dve, 6)

            def rstd_of(v, eps_col, o, w):
                link(g.tensor_tensor(o, v, half[:, eps_col:eps_col + 1].to_broadcast((P, w)), ALU.add))
                return g.tensor_tensor(o, o, half[:, 0:1].to_broadcast((P, w)), ALU.pow)

            def a_body(i):
                for u in range(2):
                    n = 2 * i + u
                    tok = bass.ds(n * P, P)
                    pool.wait_ge(a_s2, free(n, 2))
                    for gr in range(2):
                        g.tensor_tensor(qm[:, u, gr], QT[:, gr, tok].rearrange("p (o t) -> p o t", o=1).to_broadcast((P, 8, P)),
                                        K("headmask").rearrange("p (h o) -> p h o", o=1).to_broadcast((P, 8, P)),
                                        ALU.mult).then_inc(a_qm, 1)
                for u in range(2):
                    n = 2 * i + u
                    pool.wait_ge(a_var, done(n))
                    rstd_of(mv[:, u, 1:2], 1, rstd[:, u:u + 1], 1).then_inc(a_rstd, 1)
            a_body.links = 2
            looped(pool, link, 0, NPAIR // 2, a_body)

            pool.wait_ge(a_x1, done(NPAIR - 1))
            g.memset(kmx[:].bitcast(F32), 0.0).then_inc(zeroed, 1)
            link(g.memset(vst[:], 0.0))
            g.memset(vst[:, :, :, :, :, XD:XD + 1], 1.0).then_inc(zeroed, 1)

            def x_step(m, k):
                if k % 2 and valid(k, m, 3):
                    n = pair_of(m, k, 3)
                    for w in range(2):
                        pool.wait_ge(x_ropes, done(2 * n + w))
                        pool.wait_ge(x_lo, free(2 * n + w, 2))
                        g.tensor_tensor(roped[:, w], rope[:, w, 0], rope[:, w, 1], ALU.add).then_inc(x_roped, 1)
                    for w in range(2):
                        pool.wait_ge(x_hi, done(2 * n + w))
                        g.tensor_tensor(hilo[:, ((k + 3) // 2) % 2, w, 1], roped[:, w], hilo[:, ((k + 3) // 2) % 2, w, 0].bitcast(F32),
                                        ALU.subtract).then_inc(x_lo, 1)
                if k % 2 == 0 and valid_pair(m, k, -2):
                    n = pair_of(m, k, -2)
                    pool.wait_ge(x_var, done(n))
                    rstd_of(mv[:, 0, 1:2], 1, rstd[:, 0:1], 1).then_inc(x_rstd, 1)
            x_step.links = 2
            x_steps(pool, link, x_step)

            pool.wait_ge(f_ms, done(0))
            rstd_of(fpow[:], 2, rr[:], NPAIR).then_inc(f_r, 1)
            pool.wait_ge(f_wrow, 16)
            for e in range(NE):
                pool.wait_ge(f_act, free(2 * e + 3, 4))
                g.partition_broadcast(wb[:, e % 2, :], wrow[0:1, e, :]).then_inc(f_wb, 1)
            for t in range(NPAIR):
                pool.wait_ge(f_var, done(t))
                rstd_of(mv[:, t % 2, 1:2], 1, rstd[:, t % 2:t % 2 + 1], 1).then_inc(f_rstd, 1)

        @block.scalar
        def _(sc):
            a = nc.scalar
            link = Chain(sc, act_link)
            evac_phase0(sc, lambda o, i: a.copy(o, i), p0_act, 0)
            sc.wait_ge(p0_dve, 6)
            sc.wait_ge(p0_act, 6)
            sc.wait_ge(vbd_zero, 1)
            sc.wait_ge(credited, 1)

            def a_body(i):
                for u in range(2):
                    n = 2 * i + u
                    tok = bass.ds(n * P, P)
                    sc.wait_ge(a_s2, free(n, 2))
                    a.copy(qst[:, u], QT[:, :, tok]).then_inc(a_st, 1)
                    a.copy(kst[:, u], KT[:, :, tok]).then_inc(a_st, 1)
                    sc.wait_ge(a_pv, free(n, 2))
                    for b in range(2):
                        r = slice(64 * b, 64 * b + 64)
                        last = a.copy(vbd[r, u, :, b, 0:HD], V[r, bass.ds(n, 1), :].rearrange("p o (h d) -> p (o h) d", h=H))
                    last.then_inc(a_vbd, 1)
                for u in range(2):
                    n = 2 * i + u
                    sc.wait_ge(a_s2, done(n))
                    sc.wait_ge(a_pv, free(n, 2))
                    a.activation(pt[:, u].rearrange("p h q -> p (h q)"), bank[:, 2:4, :].rearrange("p a b -> p (a b)"),
                                 ACT.Exp, scale=float(HD) ** -0.5).then_inc(a_pt, 1)
                for u in range(2):
                    n = 2 * i + u
                    sc.wait_ge(a_t, done(n))
                    sc.wait_ge(a_y, free(n, 2))
                    a.copy(ot[:, u].rearrange("p h b q -> p b h q"),
                           bank[:, 5, 0:256].rearrange("p (b h q) -> p b h q", b=2, h=2)).then_inc(a_ot, 1)
            a_body.links = 0
            looped(sc, link, 0, NPAIR // 2, a_body)

            sc.wait_ge(a_x1, done(NPAIR - 1))
            sc.wait_ge(ld_ctx, 16 * 5)

            def evac_m(m, k, gr):
                sc.wait_ge(x_mt, done(2 * m + gr))
                wait_mrow_free(sc, m, k, gr)
                a.copy(mrow[:, k % 2, gr, :], bank[0:4, 2, 0:256]).then_inc(x_mte, 1)

            def x_step(m, k):
                for t in range(8):
                    if valid(k, m, 0):
                        i = 8 * m + t
                        sc.wait_ge(x_s2, done(i))
                        if t % 4 == 0:
                            sc.wait_ge(x_pv, free(2 * m + t // 4, 2))
                        a.activation(px[:, t // 4, t % 4].rearrange("p c q -> p (c q)"), bank[:, 5 + t % 2, :], ACT.Exp,
                                     scale=float(XD) ** -0.5).then_inc(x_exp, 1)
                    if t == 1 and valid(k, m, 0):
                        evac_m(m, k, 1)
                    if t == 3 and valid(k, m, 2):
                        s = (k + 2) % 4
                        for w in range(2):
                            sc.wait_ge(x_spread, done(2 * (m + 2) + w))
                            if w == 0:
                                sc.wait_ge(x_s2, free(8 * (m + 2) + 7, 32))
                                a.copy(qx[:, s], bank[:, 0, :].rearrange("p (g q) -> p g q", g=2)).then_inc(x_stack, 1)
                            else:
                                wait_km_staged(sc, m, k)
                                a.activation(kstage[:, k % 2], bank[:, 1, :].rearrange("p (g q) -> p g q", g=2),
                                             ACT.Identity, bias=K("onescol")).then_inc(x_stack, 1)
                    if t == 2 and k % 2 and valid(k, m, 1):
                        n = pair_of(m, k, 1)
                        sc.wait_ge(x_v, free(n, 1))
                        a.copy(cst[:], cx[:, bass.ds(n, 1), :].rearrange("p o d -> p (o d)")).then_inc(x_cst, 1)
                    if t == 5 and k % 2 and valid(k, m, 3):
                        n = pair_of(m, k, 3)
                        for w in range(2):
                            sc.wait_ge(x_roped, done(2 * n + w))
                            sc.wait_ge(x_spread, free(4 * n + 3, 8))
                            a.copy(hilo[:, ((k + 3) // 2) % 2, w, 0], roped[:, w]).then_inc(x_hi, 1)
                    if t == 6 and valid(k, m, 1):
                        evac_m(m + 1, k + 1, 0)
            x_step.links = 0
            x_steps(sc, None, x_step)

            sc.wait_ge(x_x2, done(NPAIR - 1))
            for t in range(NPAIR):
                if t:
                    sc.wait_ge(f_sq, done(t - 1))
                a.activation(sq[:], x_sb[:, t, :], ACT.Square, accum_out=ms[:, t:t + 1]).then_inc(f_sq, 1)
            for q in range(4):
                sc.wait_ge(f_tp, done(q))
                a.copy(hT[:, q // 2, 512 * (q % 2):512 * (q % 2) + 512], bank[:, q, :]).then_inc(f_hT, 1)
            sc.wait_ge(f_lsub, done(0))
            a.activation(ex[:], lg[:], ACT.Exp).then_inc(f_exp, 1)
            sc.wait_ge(f_wtp, done(0))
            a.copy(wT[:], bank[0:NE, 5:7, :].rearrange("p a b -> p (a b)")).then_inc(f_wT, 1)
            for i in range(2 * (NE + 1)):
                sc.wait_ge(f_gu, done(i))
                sc.wait_ge(f_prod, free(i, 2))
                a.activation(sl[:, i % 2], bank[:, 2 * (i % 2), :], ACT.Silu).then_inc(f_silu, 1)

        @block.vector
        def _(ve):
            v = nc.vector
            link = Chain(ve, dve_link)
            link(v.memset(vbd[:], 0.0))
            v.memset(vbd[0:64, :, :, 0, HD:HD + 1], 1.0)
            v.memset(vbd[64:128, :, :, 1, HD:HD + 1], 1.0).then_inc(vbd_zero, 1)
            evac_phase0(ve, lambda o, i: v.tensor_copy(o, i), p0_dve, 1)
            ve.wait_ge(ld_c, 16)
            v.tensor_copy(sel_r[:].rearrange("p a b -> p (a b)"), K("sel"))
            v.tensor_copy(sameb_r[:], K("sameb")).then_inc(consts_ready, 1)
            ve.wait_ge(ld_ctx, 16 * 5)
            for n in (1, 3):
                link(v.tensor_tensor(xw[:, n], xw[:, n], K("signrow"), ALU.mult))
                link(v.tensor_tensor(xb[:, n:n + 1], xb[:, n:n + 1], K("signcol"), ALU.mult))
            ve.wait_ge(p0_act, 6)
            ve.wait_ge(p0_dve, 6)
            ve.wait_ge(credited, 1)
            ve.wait_ge(ld_xn, 32)

            def headmasks(n, u):
                tok = bass.ds(n * P, P)
                ve.wait_ge(a_s1, free(n, 2))
                for gr in range(2):
                    v.tensor_tensor(km[:, u, gr], KT[:, gr, tok].rearrange("p (o t) -> p o t", o=1).to_broadcast((P, 8, P)),
                                    K("headmask").rearrange("p (h o) -> p h o", o=1).to_broadcast((P, 8, P)),
                                    ALU.mult).then_inc(a_km, 1)

            def layer_norm(src, u, sem_var, sem_rstd, n, o, bn_n):
                v.bn_stats(stats[:, u], src).then_inc(bn_done, 1)
                ve.wait_ge(bn_done, done(bn_n))
                v.memset(wait_here[:], 0.0)
                v.bn_aggr(mv[:, u], stats[:, u]).then_inc(sem_var, 1)
                ve.wait_ge(sem_rstd, done(n))
                return v.tensor_scalar(o, src, mv[:, u, 0:1], rstd[:, u:u + 1], ALU.subtract, ALU.mult)

            def a_body(i):
                for u in range(2):
                    headmasks(2 * i + u, u)
                for u in range(2):
                    n = 2 * i + u
                    ve.wait_ge(a_s1, done(n))
                    link(v.tensor_reduce(negmax[:, u], bank[:, 0:2, :].rearrange("p a (h k) -> p (a h) k", k=C), AX.X, ALU.max,
                                         negate=True))
                    ve.wait_ge(a_s2, free(n, 2))
                    v.tensor_tensor(shift[:, u], K("fold").rearrange("p (o q) -> p o q", o=1).to_broadcast((P, H, C)),
                                    negmax[:, u].rearrange("p (h o) -> p h o", o=1).to_broadcast((P, H, C)),
                                    ALU.mult).then_inc(a_shift, 1)
                for u in range(2):
                    n = 2 * i + u
                    ve.wait_ge(a_pv, done(n))
                    o = bank[:, 4, 0:8 * 2 * (HD + 1)].rearrange("p (h b d) -> p h b d", h=8, b=2)
                    link(v.reciprocal(rsum[:, u], o[:, :, :, HD]))
                    ve.wait_ge(a_t, free(n, 2))
                    for b in range(2):
                        last = v.tensor_tensor(on[:, u, b], o[:, :, b, 0:HD],
                                               rsum[:, u, :, b:b + 1].to_broadcast((P, 8, HD)), ALU.mult)
                    last.then_inc(a_on, 1)
                for u in range(2):
                    n = 2 * i + u
                    ve.wait_ge(a_y, done(n))
                    xs = x_sb[:, bass.ds(n, 1), :].rearrange("p o d -> p (o d)")
                    ins = v.tensor_tensor(ysum[:, u], bank[:, 6 + u, 0:D], xs, ALU.add)
                    ins.then_inc(a_sum, 1)
                    ve.wait_ge(a_sum, done(n))
                    layer_norm(ysum[:, u], u, a_var, a_rstd, n, xs, n).then_inc(a_x1, 1)
            a_body.links = 4
            looped(ve, link, 0, NPAIR // 2, a_body)

            ve.wait_ge(zeroed, 2)

            def x_step(m, k):
                for t in range(8):
                    if valid(k, m, 1):
                        ve.wait_ge(x_s1, done(8 * (m + 1) + t))
                        if t % 4 == 0:
                            ve.wait_ge(x_mt, free(2 * (m + 1) + t // 4, 4))
                        v.tensor_reduce(nmax[:, (k + 1) % 2, t // 4, (t // 2) % 2, 2 * (t % 2):2 * (t % 2) + 2],
                                        bank[:, 3 + t % 2, :].rearrange("p (h k) -> p h k", h=2), AX.X, ALU.max,
                                        negate=True).then_inc(x_max, 1)
                    if t == 2 and valid(k, m, -1):
                        s = (k - 1) % 2
                        ve.wait_ge(x_pv, done(2 * (m - 1) + 1))
                        link(v.transpose(tn[:, s].rearrange("p a b -> p (a b)"), bank[:, 7, :]))
                        link(v.reciprocal(rs[:, s], tn[:, s, :, XD]))
                        link(v.tensor_tensor(tn[:, s, :, 0:XD], tn[:, s, :, 0:XD],
                                             rs[:, s].rearrange("p (a o) -> p a o", o=1).to_broadcast((P, 16, XD)), ALU.mult))
                        v.transpose(onx[:, (k - 1) % 4].rearrange("p g q -> p (g q)"),
                                    tn[:, s].rearrange("p a b -> p (a b)")).then_inc(x_norm, 1)
                    if t == 4 and k % 2 and valid(k, m, 3):
                        n = pair_of(m, k, 3)
                        for w in range(2):
                            ve.wait_ge((x_pq, x_pk)[w], done(n))
                            ve.wait_ge(x_roped, free(2 * n + w, 2))
                            for r in range(2):
                                last = v.scalar_tensor_tensor(rope[:, w, r], bank[:, w, 256 * r:256 * r + 256],
                                                              xb[:, 2 * w + r:2 * w + r + 1], K(("cos", "sin")[r]), ALU.add, ALU.mult)
                            last.then_inc(x_ropes, 1)
                    if t == 5 and k % 2 and valid(k, m, 1):
                        n = pair_of(m, k, 1)
                        ve.wait_ge(x_v, done(n))
                        ve.wait_ge(x_pv, free(4 * n + 3, 8))
                        for c in range(2):
                            for b in range(2):
                                last = v.tensor_tensor(vst[:, ((k + 1) // 2) % 2, c, b, :, 0:XD],
                                                       bank[:, 2, P * c + 64 * b:P * c + 64 * b + 64].rearrange("p (h d) -> p h d", h=XH),
                                                       bvb[:].rearrange("p (h d) -> p h d", h=XH), ALU.add)
                        last.then_inc(x_vst, 1)
                    if t == 5 and k % 2 == 0 and valid_pair(m, k, -2):
                        n = pair_of(m, k, -2)
                        ve.wait_ge(x_y, done(n))
                        xs = x_sb[:, bass.ds(n, 1), :].rearrange("p o d -> p (o d)")
                        v.scalar_tensor_tensor(ysum[:, 0], bank[:, 2, 0:D], xb[:, 4:5], xs, ALU.add, ALU.add).then_inc(x_ysum, 1)
                        ve.wait_ge(x_ysum, done(n))
                        layer_norm(ysum[:, 0], 0, x_var, x_rstd, n, xs, NPAIR + n).then_inc(x_x2, 1)
            x_step.links = 3 * 4
            x_steps(ve, link, x_step)

            ve.wait_ge(f_sq, done(NPAIR - 1))
            ve.wait_ge(ld_f, 16 * 4)
            v.tensor_scalar(fpow[:], ms[:], 1.0 / D, None, ALU.mult).then_inc(f_ms, 1)
            ve.wait_ge(f_r, done(0))
            for t in range(NPAIR):
                v.scalar_tensor_tensor(hh[:, t], x_sb[:, t], rr[:, t:t + 1], rmsw[:], ALU.mult, ALU.mult).then_inc(f_h, 1)
            ve.wait_ge(f_lg, done(0))
            lps = bank[:, 4, 0:NPAIR * NE].rearrange("p (t e) -> p t e", e=NE)
            link(v.tensor_reduce(lmax[:], lps, AX.X, ALU.max))
            link(v.tensor_tensor(lg[:], lps, lmax[:].rearrange("p (t o) -> p t o", o=1).to_broadcast((P, NPAIR, NE)), ALU.subtract))
            v.engine_nop() if False else None
            self_l = [lg[:, t].rearrange("p (i o) -> p i o", o=1).to_broadcast((P, NE, NE)) for t in range(NPAIR)]
            other_l = [lg[:, t].rearrange("p (o j) -> p o j", o=1).to_broadcast((P, NE, NE)) for t in range(NPAIR)]
            for t in range(NPAIR):
                v.tensor_tensor(gt[:, t], other_l[t], self_l[t], ALU.is_gt)
                last = v.tensor_tensor(eq[:, t], other_l[t], self_l[t], ALU.is_equal)
            last.then_inc(f_lsub, 1)
            ve.wait_ge(f_lsub, done(0))
            before = K("before").rearrange("p (o n) -> p o n", o=1).to_broadcast((P, NPAIR, NE * NE))
            link(v.tensor_tensor(eq[:].rearrange("p t i j -> p t (i j)"), eq[:].rearrange("p t i j -> p t (i j)"), before, ALU.mult))
            link(v.tensor_tensor(gt[:], gt[:], eq[:], ALU.add))
            link(v.tensor_reduce(rank[:], gt[:], AX.X, ALU.add))
            ve.wait_ge(f_exp, done(0))
            link(v.scalar_tensor_tensor(wsel[:], rank[:], 2.0, ex[:], ALU.is_lt, ALU.mult))
            link(v.tensor_reduce(wsum[:], wsel[:], AX.X, ALU.add))
            link(v.reciprocal(lmax[:], wsum[:]))
            v.tensor_tensor(wsel[:], wsel[:], lmax[:].rearrange("p (t o) -> p t o", o=1).to_broadcast((P, NPAIR, NE)),
                            ALU.mult).then_inc(f_w, 1)
            for i in range(2 * (NE + 1)):
                e, hf = order(i)
                ve.wait_ge(f_silu, done(i))
                ve.wait_ge(f_dn, free(i, 2))
                dst = act[:, i % 2] if e == NE else pr[:, i % 2]
                v.tensor_tensor(dst, bank[:, 2 * (i % 2) + 1, :], sl[:, i % 2], ALU.mult).then_inc(f_prod, 1)
                if e == NE:
                    ve.wait_ge(f_prod, done(i))
                    v.engine_nop().then_inc(f_act, 1) if False else ve.sem_inc(f_act, 1)
                else:
                    ve.wait_ge(f_prod, done(i))
                    ve.wait_ge(f_wb, done(e))
                    v.tensor_tensor(act[:, i % 2], pr[:, i % 2], wb[:, e % 2, 512 * hf:512 * hf + 512], ALU.mult).then_inc(f_act, 1)
            for t in range(NPAIR):
                if t == 0:
                    ve.wait_ge(f_dn, done(2 * NE + 1))
                link(v.tensor_tensor(fy[:, t % 2], bank[:, 4 + t // 2, 256 * (t % 2):256 * (t % 2) + 256], x_sb[:, t], ALU.add))
                if t >= 2:
                    ve.wait_ge(st_out[t % 2], 16 * (t // 2))
                layer_norm(fy[:, t % 2], t % 2, f_var, f_rstd, t, fo[:, t % 2], 2 * NPAIR + t).then_inc(f_o, 1)

        @block.tensor
        def _(pe):
            mm = nc.tensor.matmul
            pe.wait_ge(ld_w, 16)
            pe.wait_ge(ld_x, 32)
            for n in range(12):
                if n >= 8:
                    pe.wait_ge((p0_act, p0_dve)[n % 2], (n - 8) // 2 + 1)
                for part in range(1 if n < 8 else 2):
                    for c in range(2):
                        if n < 8:
                            w, gr, hf = n // 4, (n // 2) % 2, n % 2
                            last = mm(bank[:, n, :], wqkv[:, w, c, P * gr:P * gr + P], xT[:, c, 512 * hf:512 * hf + 512],
                                      start=c == 0, stop=c == 1)
                        else:
                            t = 2 * (n - 8) + part
                            last = mm(bank[:, n % 8, D * part:D * part + D], xT[:, c, P * t:P * t + P], wqkv[:, 2, c, :],
                                      start=c == 0, stop=c == 1)
                last.then_inc(p0_mm, 1)
            pe.wait_ge(p0_act, 6)
            pe.wait_ge(p0_dve, 6)
            pe.wait_ge(consts_ready, 1)
            pe.wait_ge(credited, 1)
            pe.wait_ge(ld_xn, 32)

            def a_body(i):
                for u in range(2):
                    n = 2 * i + u
                    pe.wait_ge(a_st, done(2 * n + 1))
                    pe.wait_ge(a_km, done(2 * n + 1))
                    pe.wait_ge(a_shift, free(n, 1))
                    for gr in range(2):
                        for b in range(2):
                            t = slice(64 * b, 64 * b + 64)
                            last = mm(bank[t, gr, :], qst[:, u, gr, t], km[:, u, gr, :, t], start=True, stop=True)
                    last.then_inc(a_s1, 1)
                for u in range(2):
                    n = 2 * i + u
                    pe.wait_ge(a_shift, done(n))
                    pe.wait_ge(a_qm, done(2 * n + 1))
                    pe.wait_ge(a_pt, free(n, 1))
                    for gr in range(2):
                        mm(bank[:, 2 + gr, :], sameb_r[:], shift[:, u, 8 * gr:8 * gr + 8, :], start=True, stop=False, skip_group_check=True)
                        for b in range(2):
                            t = slice(64 * b, 64 * b + 64)
                            last = mm(bank[t, 2 + gr, :], kst[:, u, gr, t], qm[:, u, gr, :, t], start=False, stop=True,
                                      skip_group_check=True)
                    last.then_inc(a_s2, 1)
                for u in range(2):
                    n = 2 * i + u
                    pe.wait_ge(a_pt, done(n))
                    pe.wait_ge(a_vbd, done(n))
                    pe.wait_ge(a_on, free(n, 1))
                    for h in range(H):
                        o = 34 * (h // 2)
                        last = mm(bank[64 * (h % 2):64 * (h % 2) + 64, 4, o:o + 34], pt[:, u, h, :],
                                  vbd[:, u, h].rearrange("p b d -> p (b d)"), start=True, stop=True, skip_group_check=True)
                    last.then_inc(a_pv, 1)
                for u in range(2):
                    n = 2 * i + u
                    pe.wait_ge(a_on, done(n))
                    pe.wait_ge(a_ot, free(n, 1))
                    for b in range(2):
                        last = nc.tensor.transpose(bank[:, 5, P * b:P * b + P], on[:, u, b].rearrange("p h d -> p (h d)"), K("ident"))
                    last.then_inc(a_t, 1)
                    pe.wait_ge(a_ot, done(n))
                    pe.wait_ge(a_x1, free(n, 2))
                    for h2 in range(2):
                        last = mm(bank[:, 6 + u, 0:D], ot[:, u, h2].rearrange("p b q -> p (b q)"), wo[:, h2, :], start=h2 == 0, stop=h2 == 1)
                    last.then_inc(a_y, 1)
            with pe.Fori(0, NPAIR // 2) as i:
                a_body(i)

            pe.wait_ge(a_x1, done(NPAIR - 1))
            pe.wait_ge(ld_ctx, 16 * 5)
            pe.wait_ge(zeroed, 2)

            def maxima_rows(m, k, gr):
                pe.wait_ge(x_max, done(8 * m + 4 * gr + 3))
                free_bank2(pe, m, k, gr)
                for c in range(2):
                    last = nc.tensor.transpose(bank[0:4, 2, P * c:P * c + P], nmax[:, k % 2, gr, c, :], K("ident"))
                last.then_inc(x_mt, 1)

            def weighted_values(m, k, gr):
                pe.wait_ge(x_exp, done(8 * m + 4 * gr + 3))
                if gr == 0:
                    pe.wait_ge(x_vst, done(pair_floor(m, k)))
                    pe.wait_ge(x_norm, free(m, 1))
                for c in range(2):
                    for j in range(4):
                        last = mm(bank[XROW * j:XROW * j + XROW, 7, D * gr:D * gr + D], vst[:, (k // 2) % 2, c, k % 2, 4 * gr + j, :],
                                  px[:, gr, j, c, :], start=c == 0, stop=c == 1, skip_group_check=True)
                last.then_inc(x_pv, 1)

            def x_step(m, k):
                for t in range(8):
                    if valid(k, m, 1):
                        m1, s = m + 1, (k + 1) % 4
                        gr, c, hp = t // 4, (t // 2) % 2, t % 2
                        if t == 0:
                            pe.wait_ge(x_stack, done(2 * m1))
                            wait_km(pe, m1, k + 1)
                        pe.wait_ge(x_max, free(8 * m1 + t, 2))
                        mm(bank[:, 3 + t % 2, :], qx[:, s, gr, P * c:P * c + P],
                           kmx[:, s, 4 * gr + 2 * hp:4 * gr + 2 * hp + 2, :].rearrange("p h k -> p (h k)"),
                           start=True, stop=True).then_inc(x_s1, 1)
                    if valid(k, m, 0):
                        s, gr = k % 4, t // 4
                        if t % 4 == 0:
                            wait_mrow(pe, m, k, gr)
                        pe.wait_ge(x_exp, free(8 * m + t, 2))
                        for c in range(2):
                            last = mm(bank[:, 5 + t % 2, D * c:D * c + D], kmx[:, s, t, P * c:P * c + P], qx[:, s, gr, :],
                                      start=True, stop=True, skip_group_check=True)
                        last.then_inc(x_s2, 1)
                    if t == 1:
                        if valid(k, m, 0):
                            maxima_rows(m, k, 1)
                        if valid(k, m, -1):
                            weighted_values(m - 1, k - 1, 1)
                    if t == 2 and valid(k, m, 2):
                        n = pair_floor2(m, k)
                        b = k % 2
                        sl_ = ((k + 2) // 2) % 2
                        for w in range(2):
                            pe.wait_ge(x_lo, done(2 * n + w))
                            pe.wait_ge(x_stack, free(2 * (m + 2) + w, 2))
                            for gr in range(2):
                                for part in range(2):
                                    last = mm(bank[:, w, D * gr:D * gr + D], sel_r[:, ((w * 2 + b) * 2 + gr) * 2 + part, :],
                                              hilo[:, sl_, w, part, :], start=part == 0, stop=part == 1, skip_group_check=True)
                            last.then_inc(x_spread, 1)
                    if t == 3 and k % 2 and valid(k, m, 3):
                        n = pair_of(m, k, 3)
                        for w in range(2):
                            pe.wait_ge(x_stack, free(4 * n + w, 2))
                            src = (x_sb, cx)[w][:, bass.ds(n, 1), :].rearrange("p o d -> p (o d)")
                            for r in range(2):
                                last = mm(bank[:, w, D * r:D * r + D], xw[:, 2 * w + r, :], src, start=True, stop=True,
                                          skip_group_check=True)
                            last.then_inc((x_pq, x_pk)[w], 1)
                    if t == 4 and k % 2 and valid(k, m, 1):
                        n = pair_of(m, k, 1)
                        pe.wait_ge(x_cst, done(n))
                        free_bank2_v(pe, m, k)
                        for c in range(2):
                            last = mm(bank[:, 2, P * c:P * c + P], cst[:, P * c:P * c + P], xw[:, 4, :], start=True, stop=True,
                                      skip_group_check=True)
                        last.then_inc(x_v, 1)
                    if t == 4 and k % 2 == 0 and valid_pair(m, k, -2):
                        n = pair_of(m, k, -2)
                        pe.wait_ge(x_norm, done(2 * n + 1))
                        free_bank2_v(pe, m, k)
                        for gr in range(2):
                            for b in range(2):
                                last = mm(bank[64 * b:64 * b + 64, 2, 0:D], xwo[:, gr, :], onx[:, (k - 2 + b) % 4, gr, :],
                                          start=gr == 0, stop=gr == 1, skip_group_check=True)
                        last.then_inc(x_y, 1)
                    if t == 5 and valid(k, m, 1):
                        maxima_rows(m + 1, k + 1, 0)
                    if t == 6 and valid(k, m, 0):
                        weighted_values(m, k, 0)

            x_steps(pe, None, x_step)

            pe.wait_ge(ld_f, 16 * 4)
            for q in range(4):
                c, hf = q // 2, q % 2
                for t in range(4 * hf, 4 * hf + 4):
                    pe.wait_ge(f_h, done(t))
                    last = nc.tensor.transpose(bank[:, q, P * (t % 4):P * (t % 4) + P], hh[:, t, P * c:P * c + P], K("ident"))
                last.then_inc(f_tp, 1)
            pe.wait_ge(f_hT, done(3))
            for t in range(NPAIR):
                for c in range(2):
                    last = mm(bank[:, 4, NE * t:NE * t + NE], hT[:, c, P * t:P * t + P], rw[:, c, :], start=c == 0, stop=c == 1,
                              skip_group_check=True)
            last.then_inc(f_lg, 1)

            def gate_up(i):
                e, hf = order(i)
                pe.wait_ge(f_prod, free(i, 2))
                for u in range(2):
                    for c in range(2):
                        last = mm(bank[:, 2 * (i % 2) + u, :], wgu[:, e, u, c, :], hT[:, c, 512 * hf:512 * hf + 512],
                                  start=c == 0, stop=c == 1)
                last.then_inc(f_gu, 1)

            def down(i):
                e, hf = order(i)
                pe.wait_ge(f_act, done(i))
                for t in range(4):
                    tt = 4 * hf + t
                    last = mm(bank[:, 4 + tt // 2, D * (tt % 2):D * (tt % 2) + D], act[:, i % 2, P * t:P * t + P], wdn[:, e, :],
                              start=(i < 2 and tt % 2 == 0), stop=(i >= 2 * NE), skip_group_check=True)
                last.then_inc(f_dn, 1)

            gate_up(0)
            gate_up(1)
            pe.wait_ge(f_w, done(0))
            for t in range(NPAIR):
                last = nc.tensor.transpose(bank[0:NE, 5 + t // 4, P * (t % 4):P * (t % 4) + P], wsel[:, t, :], K("ident"))
            last.then_inc(f_wtp, 1)
            pe.wait_ge(f_wT, done(0))
            for i in range(2 * (NE + 1)):
                down(i)
                if i + 2 < 2 * (NE + 1):
                    gate_up(i + 2)

def kernel(**inp):
    import concourse.bacc as bacc
    from concourse.bass_utils import run_bass_kernel_spmd

    def arr(a):
        return np.ascontiguousarray(np.asarray(a))

    a = {k: arr(v) for k, v in inp.items()}
    partner = np.arange(C) ^ (XD // 2)
    evenodd = np.concatenate([np.arange(HD) + HD * h for h in list(range(0, H, 2)) + list(range(1, H, 2))])
    x2d = a["x"].reshape(NTOK, D)
    chunks = lambda w: w.reshape(2, P, -1).transpose(1, 0, 2)

    def twice(w):
        z = np.zeros((P, P), w.dtype)
        z[:C, :C] = z[C:, C:] = w
        return z

    def spread(w):
        z = np.zeros((P, 2, C), w.dtype)
        for h in range(XH):
            r = XROW * (h % 4)
            z[r:r + XD, h // 4] = w[XD * h:XD * h + XD]
        return z

    qT, kT, vT, oT = (a["L0_xattn_W" + n].T for n in "qkvo")
    bq, bk, bo = (a["L0_xattn_b" + n] for n in "qko")
    gate = np.concatenate([a["L0_ffn_w_gate"], a["L0_ffn_sw_gate"][None]])
    up = np.concatenate([a["L0_ffn_w_up"], a["L0_ffn_sw_up"][None]])
    down = np.concatenate([a["L0_ffn_w_down"], a["L0_ffn_sw_down"][None]])
    A = {
        "x": x2d, "xT": x2d.T, "ctx": a["ctx_2048"].reshape(NTOK, D),
        "wqkv": np.stack([chunks(a["L0_attn_W" + n].T) for n in "qkv"], axis=1),
        "wo": chunks(a["L0_attn_Wo"].T[evenodd]),
        "xw": np.stack([twice(w) for w in (qT, qT[:, partner], kT, kT[:, partner], vT)], axis=1),
        "xwo": spread(oT),
        "xb": np.stack([np.tile(w, 2) for w in (bq, bq[partner], bk, bk[partner], bo)], axis=1),
        "xbv": a["L0_xattn_bv"], "rms": a["L0_ffn_rms_weight"],
        "wgu": np.stack([gate, up], axis=1).reshape(NE + 1, 2, 2, P, F).transpose(3, 0, 1, 2, 4),
        "wdn": down.transpose(1, 0, 2),
        "rw": chunks(a["L0_ffn_router_w"]),
        "con": constant_block()[0],
    }
    nc = bacc.Bacc("TRN2", target_bir_lowering=False, num_devices=1)
    arrays, aps = {}, {}
    for name, v in A.items():
        v = np.ascontiguousarray(v)
        arrays["in_" + name] = v
        aps[name] = nc.dram_tensor("in_" + name, v.shape, mybir.dt.from_np(v.dtype), kind="ExternalInput").ap()
    out = nc.dram_tensor("out_y", (NTOK, D), F32, kind="ExternalOutput").ap()
    build(nc, aps, out)
    r = run_bass_kernel_spmd(nc, [arrays], core_ids=[0])
    return r.results[0]["out_y"].reshape(B, C, D)
```

```python
from contextlib import ExitStack

import numpy as np
import concourse.bass as bass
from concourse import mybir

F32 = mybir.dt.float32
F32R = mybir.dt.float32r
ALU = mybir.AluOpType
ACT = mybir.ActivationFunctionType
AX = mybir.AxisListType

P = 128
B, C, D = 16, 64, 256
NTOK = B * C
NPAIR = B // 2
H, HD = 16, 16
XH, XD = 8, 8
NE, F = 8, 128
LN_EPS, RMS_EPS = 1e-5, 1e-6
XROW = 32
MAXROW = 24
CREDIT = 32


def done(n):
    return n + 1 + CREDIT


def free(n, depth):
    return n + 1 + CREDIT - depth


def constant_block():
    p = np.arange(P)
    blocks = {}
    blocks["ident"] = np.eye(P)
    inv = (np.float32(1.0) / np.power(np.float32(10000.0), np.arange(0, XD, 2, dtype=np.float32) / np.float32(XD))).astype(np.float32)
    ang = (np.arange(D, dtype=np.float32)[:, None] * inv[None, :]).astype(np.float32)
    ang = np.concatenate([ang, ang], axis=1)
    blocks["cos"] = np.cos(ang).T[p % XD]
    blocks["sin"] = np.sin(ang).T[p % XD]
    blocks["signrow"] = np.broadcast_to(np.where(p % XD < XD // 2, -1.0, 1.0), (P, P))
    blocks["signcol"] = np.where(p % XD < XD // 2, -1.0, 1.0)[:, None]
    blocks["headmask"] = (p[:, None] // HD == np.arange(8)[None, :])
    blocks["fold"] = (p[:, None] % C == np.arange(C)[None, :])
    blocks["sameb"] = (p[:, None] // C == p[None, :] // C)
    blocks["onescol"] = (p % XROW == MAXROW)[:, None]
    blocks["before"] = np.broadcast_to((np.arange(NE)[None, :] < np.arange(NE)[:, None]).reshape(1, NE * NE), (P, NE * NE))
    sel = np.zeros((P, 2, 2, 2, 2, P))
    for w, parts in enumerate(((0, 0, 1), (0, 1, 0))):
        for b in range(2):
            for h in range(XH):
                for c, part in enumerate(parts):
                    for d in range(XD):
                        sel[64 * b + XD * h + d, w, b, h // 4, part, XROW * (h % 4) + XD * c + d] = 1
    at, cols = {}, 0
    for k, v in blocks.items():
        at[k] = (cols, cols + v.shape[1])
        cols += v.shape[1]
    return np.concatenate([np.asarray(v, np.float32) for v in blocks.values()], axis=1), at, sel.reshape(P, -1).astype(np.float32)


def build(nc, I, out):
    _, CAT, _ = constant_block()
    ncon = max(v[1] for v in CAT.values())
    ctx = ExitStack()
    with ctx:
        def sb(name, shape, dt=F32):
            return ctx.enter_context(nc.sbuf_tensor("b_" + name, shape, dt))

        def sem(name):
            return ctx.enter_context(nc.semaphore(name))

        bank = ctx.enter_context(nc.psum_tensor("bank", [P, 8, 512], F32))
        con = sb("con", [P, ncon])
        K = lambda k: con[:, CAT[k][0]:CAT[k][1]]
        x_sb = sb("x", [P, NPAIR, D])
        sel_r = sb("sel_r", [P, 16, P], F32R)
        sameb_r = sb("sameb_r", [P, P], F32R)
        cx = sb("cx", [P, NPAIR, D])
        xw = sb("xw", [P, 5, P])
        xwo = sb("xwo", [P, 2, C])
        xb = sb("xb", [P, 5])
        bvb = sb("bvb", [P, 4 * C])
        rmsw = sb("rmsw", [P, D])
        rw = sb("rw", [P, 2, P])
        rw_r = sb("rw_r", [P, 2, 2, P], F32R)
        ysum = sb("ysum", [P, 2, D])
        stats = sb("stats", [P, 2, 6])
        mv = sb("mv", [P, 2, 2])
        rstd = sb("rstd", [P, 2])
        wait_here = sb("wait_here", [P, 1])
        half = sb("half", [P, 4])
        kmx = sb("kmx", [P, 4, XH, D], F32R)
        qx = sb("qx", [P, 4, 2, D], F32R)
        kstage = sb("kstage", [P, 2, 2, D], F32R)
        rope = sb("rope", [P, 2, 2, D])
        roped = sb("roped", [P, 2, D])
        hilo = sb("hilo", [P, 2, 2, 2, D], F32R)
        cst = sb("cst", [P, D])
        vst = sb("vst", [P, 2, 2, 2, XH, XROW])
        nmax = sb("nmax", [P, 2, 2, 2, 4])
        mrow = sb("mrow", [4, 2, 2, D], F32R)

        ld_x, ld_w, ld_xn, ld_c, ld_f = sem("ld_x"), sem("ld_w"), sem("ld_xn"), sem("ld_c"), sem("ld_f")
        ld_ctx, ld_f2 = sem("ld_ctx"), sem("ld_f2")
        zeroed = sem("zeroed")
        vbd_zero = sem("vbd_zero")
        consts_ready = sem("consts_ready")
        p0_mm, p0_act, p0_dve = sem("p0_mm"), sem("p0_act"), sem("p0_dve")
        credit = {}

        def dsem(name):
            credit[name] = sem(name)
            return credit[name]

        dve_link, act_link, pool_link = sem("dve_link"), sem("act_link"), sem("pool_link")
        a_st, a_km, a_qm, a_vbd = dsem("a_st"), dsem("a_km"), dsem("a_qm"), dsem("a_vbd")
        a_s1, a_shift, a_s2, a_pt, a_pv = dsem("a_s1"), dsem("a_shift"), dsem("a_s2"), dsem("a_pt"), dsem("a_pv")
        a_on, a_t, a_ot, a_y = dsem("a_on"), dsem("a_t"), dsem("a_ot"), dsem("a_y")
        bn_done = dsem("bn_done")
        a_var, a_rstd, a_x1, a_sum = dsem("a_var"), dsem("a_rstd"), dsem("a_x1"), dsem("a_sum")
        x_pq, x_pk, x_ropes, x_roped, x_hi, x_lo, x_spread = (dsem("x_pq"), dsem("x_pk"), dsem("x_ropes"), dsem("x_roped"),
                                                     dsem("x_hi"), dsem("x_lo"), dsem("x_spread"))
        x_stack, x_cst, x_v, x_vst = dsem("x_stack"), dsem("x_cst"), dsem("x_v"), dsem("x_vst")
        x_km = [sem(f"x_km{s}") for s in range(4)]
        x_mrow = [sem(f"x_mrow{s}") for s in range(8)]
        x_s1, x_max, x_mt, x_mte = dsem("x_s1"), dsem("x_max"), dsem("x_mt"), dsem("x_mte")
        x_s2, x_exp, x_pv, x_norm = dsem("x_s2"), dsem("x_exp"), dsem("x_pv"), dsem("x_norm")
        x_n1, x_n2 = dsem("x_n1"), dsem("x_n2")
        x_y, x_ysum, x_var, x_rstd, x_x2 = dsem("x_y"), dsem("x_ysum"), dsem("x_var"), dsem("x_rstd"), dsem("x_x2")
        x_sq, x_rr, x_h, x_ht, x_hhi, x_hlo = dsem("x_sq"), dsem("x_rr"), dsem("x_h"), dsem("x_ht"), dsem("x_hhi"), dsem("x_hlo")
        f_lt, f_lte, f_lg, f_lsub, f_exp, f_w = dsem("f_lt"), dsem("f_lte"), dsem("f_lg"), dsem("f_lsub"), dsem("f_exp"), dsem("f_w")
        f_wtp, f_wT, f_wb = dsem("f_wtp"), dsem("f_wT"), dsem("f_wb")
        f_wrow = [sem("f_wrow0"), sem("f_wrow1")]
        f_whi, f_wlo, f_ahi, f_alo = dsem("f_whi"), dsem("f_wlo"), dsem("f_ahi"), dsem("f_alo")
        f_gu, f_silu, f_prod, f_act, f_dn = dsem("f_gu"), dsem("f_silu"), dsem("f_prod"), dsem("f_act"), dsem("f_dn")
        f_var, f_rstd, f_o, st_out = dsem("f_var"), dsem("f_rstd"), dsem("f_o"), sem("st_out")
        rw_ready = sem("rw_ready")
        credited = sem("credited")

        scopeA = ctx.enter_context(ExitStack())

        def sbA(name, shape, dt=F32):
            return scopeA.enter_context(nc.sbuf_tensor("a_" + name, shape, dt))

        QT = sbA("QT", [P, 2, NTOK])
        KT = sbA("KT", [P, 2, NTOK])
        V = sbA("V", [P, NPAIR, D])
        wo = sbA("wo", [P, 2, D])
        qst, kst = sbA("qst", [P, 2, 2, P]), sbA("kst", [P, 2, 2, P])
        vbd = sbA("vbd", [P, 2, H, 2, HD + 1])
        negmax = sbA("negmax", [P, 2, H])
        shift = sbA("shift", [P, 2, H, C], F32R)
        pt = sbA("pt", [P, 2, H, C])
        rsum = sbA("rsum", [P, 2, 8, 2])
        on = sbA("on", [P, 2, 2, 8, HD])
        ot = sbA("ot", [P, 2, 2, 2, C])
        scope0 = scopeA.enter_context(ExitStack())
        xT = scope0.enter_context(nc.sbuf_tensor("p_xT", [P, 2, NTOK], F32))
        wqkv = scope0.enter_context(nc.sbuf_tensor("p_wqkv", [P, 3, 2, D], F32))
        sel = scope0.enter_context(nc.sbuf_tensor("p_sel", [P, 16, P], F32))
        scope0.close()
        qm, km = sbA("qm", [P, 2, 2, 8, P]), sbA("km", [P, 2, 2, 8, P])
        scopeA.close()
        hT = sb("hT", [P, 2, 2, NTOK], F32R)
        wgu = sb("wgu", [P, NE + 1, 2, 2, F])
        wdn = sb("wdn", [P, NE + 1, D])
        scopeX = ctx.enter_context(ExitStack())

        def sbX(name, shape, dt=F32):
            return scopeX.enter_context(nc.sbuf_tensor("x_" + name, shape, dt))

        px = sbX("px", [P, 2, 4, 2, D])
        tn = sbX("tn", [P, 2, 16, 32])
        rs = sbX("rs", [P, 2, 16])
        onx = sbX("onx", [P, 4, 2, D])
        sq = sbX("sq", [P, D])
        ms = sbX("ms", [P, 2])
        rr = sbX("rr", [P, 2])
        hx = sbX("hx", [P, 2, D])
        scopeX.close()
        scopeF = ctx.enter_context(ExitStack())

        def sbF(name, shape, dt=F32):
            return scopeF.enter_context(nc.sbuf_tensor("f_" + name, shape, dt))

        kflat = kmx[:].rearrange("p s h k -> p (s h k)")
        WE = 4 * F + D
        w_r = kflat[:, 0:4 * WE].rearrange("p (s r n) -> p s r n", s=2, r=2)
        act_r = kflat[:, 4 * WE:4 * WE + 2048].rearrange("p (s r n) -> p s r n", s=2, r=2)
        lT = sbF("lT", [NE, NTOK])
        lg = sbF("lg", [P, NPAIR, NE])
        lmax = sbF("lmax", [P, NPAIR])
        ex = sbF("ex", [P, NPAIR, NE])
        gt = sbF("gt", [P, NPAIR, NE, NE])
        eq = sbF("eq", [P, NPAIR, NE, NE])
        rank = sbF("rank", [P, NPAIR, NE])
        wsel = sbF("wsel", [P, NPAIR, NE])
        wsum = sbF("wsum", [P, NPAIR])
        wrow = sbF("wrow", [1, 2, NTOK])
        wb = sbF("wb", [P, 2, NTOK])
        sl = sbF("sl", [P, 2, 512])
        pr = sbF("pr", [P, 2, 512])
        act = sbF("act", [P, 2, 512])
        fy = sbF("fy", [P, NPAIR, D])
        fstats = sbF("fstats", [P, NPAIR, 6])
        fmv = sbF("fmv", [P, NPAIR, 2])
        fvar = sbF("fvar", [P, NPAIR])
        frstd = sbF("frstd", [P, NPAIR])
        scopeF.close()
        wT = lT

        class Chain:

            def __init__(self, eng, s):
                self.eng, self.s, self.base, self.k = eng, s, 0, 0

            def __call__(self, ins):
                self.k += 1
                ins.then_inc(self.s, 1)
                self.eng.wait_ge(self.s, self.base + self.k)

            def loop(self, it, first, per):
                self.start = self.base
                self.base = self.start + self.k_before + (it - first) * per
                self.k = 0

        def looped(eng, chain, lo, hi, body):
            start = chain.base + chain.k
            per = [0]

            with eng.Fori(lo, hi) as i:
                chain.k, per_guess = 0, body.links
                chain.base = start + (i - lo) * per_guess if per_guess else start
                body(i)
                assert chain.k == per_guess, (chain.k, per_guess)
            chain.base, chain.k = start + (hi - lo) * per_guess, 0

        cur = {}

        def steps(eng, chain, step, unroll, first, lo, hi, last):
            for n in range(first, unroll * lo):
                step(n, n)
            start = chain.base + chain.k if chain else 0
            with eng.Fori(lo, hi) as j:
                cur["half"] = 2 * j
                if chain:
                    chain.base, chain.k = start + (j - lo) * step.links, 0
                for k in range(unroll):
                    step(unroll * j + k, k)
                if chain:
                    assert chain.k == step.links, chain.k
            if chain:
                chain.base, chain.k = start + (hi - lo) * step.links, 0
            for n in range(unroll * hi, last + 1):
                step(n, n)

        def valid(k, m, off, count=B):
            return (not isinstance(m, int)) or 0 <= m + off < count

        def all_steps(eng, chain, a_step, x_step, x_first, f_first):
            steps(eng, chain, a_step, 2, -1, 1, NPAIR // 2 - 1, NPAIR - 1)
            x_first()
            x_step(-4, -4)
            x_step(-3, -3)
            a_step(NPAIR, NPAIR)
            x_step(-2, -2)
            a_step(NPAIR + 1, NPAIR + 1)
            x_step(-1, -1)
            steps(eng, chain, x_step, 4, 0, 1, B // 4 - 1, B)
            f_first()
            for m in range(B + 1, B + 3):
                x_step(m, m)

        def pair_of(m, k, off):
            if isinstance(m, int):
                return (m + off) // 2
            return cur["half"] + (k + off) // 2

        def valid_pair(m, k, off):
            return (not isinstance(m, int)) or 0 <= m + off < B

        def wait_km_staged(eng, m, k):
            if isinstance(m, int):
                if m >= 0:
                    eng.wait_ge(x_km[k % 4], 64 * (m // 4 + 1))
            else:
                eng.wait_ge(x_km[k % 4], ((m - k) * 16) + 64)

        def wait_mrow_free(eng, m, k, gr):
            s = ((k - 2) % 4) * 2 + gr
            if isinstance(m, int):
                if m >= 2:
                    eng.wait_ge(x_mrow[s], 16 * ((m - 2) // 4 + 1))
            else:
                eng.wait_ge(x_mrow[s], (m - k) * 4 + 16 * ((k - 2) // 4 + 1))

        def evac_phase0(eng, copy, s, parity):
            for n in range(parity, 12, 2):
                eng.wait_ge(p0_mm, n + 1)
                if n < 8:
                    w, gr, hf = n // 4, (n // 2) % 2, n % 2
                    ins = copy((QT, KT)[w][:, gr, 512 * hf:512 * hf + 512], bank[:, n, :])
                else:
                    v = n - 8
                    ins = copy(V[:, 2 * v:2 * v + 2, :].rearrange("p a d -> p (a d)"), bank[:, n % 8, :])
                ins.then_inc(s, 1)

        def expert(ei):
            return NE if ei == 0 else ei - 1

        def order(i):
            return expert(i // 2), i % 2

        NI = 2 * (NE + 1)
        GU = (3, 5)
        ACC = (0, 1, 2, 7)

        def pair_floor(m, k):
            return m // 2 if isinstance(m, int) else cur["half"] + k // 2

        def pair_floor2(m, k):
            return (m + 2) // 2 if isinstance(m, int) else cur["half"] + (k + 2) // 2

        def wait_km(eng, m, k):
            if isinstance(m, int):
                eng.wait_ge(x_km[k % 4], 64 * (m // 4 + 1))
            else:
                eng.wait_ge(x_km[k % 4], (m - k) * 16 + 64 * (k // 4 + 1))

        def wait_mrow(eng, m, k, gr):
            s = (k % 4) * 2 + gr
            if isinstance(m, int):
                eng.wait_ge(x_mrow[s], 16 * (m // 4 + 1))
            else:
                eng.wait_ge(x_mrow[s], (m - k) * 4 + 16 * (k // 4 + 1))

        def s2_tile(m, k, t):
            return (m, k, t - 2) if t >= 2 else (m - 1, k - 1, t + 6)

        block = ctx.enter_context(nc.Block())

        @block.sync
        def _(sp):
            sp.dma_start(xT[:, :, 0:512], I["xT"].rearrange("(c p) t -> p c t", p=P)[:, :, 0:512]).then_inc(ld_x, 16)
            sp.dma_start(wqkv[:], I["wqkv"]).then_inc(ld_w, 16)
            sp.dma_start(xT[:, :, 512:1024], I["xT"].rearrange("(c p) t -> p c t", p=P)[:, :, 512:1024]).then_inc(ld_x, 16)
            sp.dma_start(con[:, :], I["con"]).then_inc(ld_c, 16)
            sp.dma_start(sel[:].rearrange("p a b -> p (a b)"), I["sel"]).then_inc(ld_c, 16)
            sp.dma_start(wo[:], I["wo"]).then_inc(ld_xn, 16)
            sp.dma_start(x_sb[:], I["x"].rearrange("(n p) d -> p n d", p=P)).then_inc(ld_xn, 16)
            sp.dma_start(cx[:], I["ctx"].rearrange("(n p) d -> p n d", p=P)).then_inc(ld_ctx, 16)
            for o, name in ((xw, "xw"), (xwo, "xwo"), (xb, "xb")):
                sp.dma_start(o[:], I[name]).then_inc(ld_ctx, 16)
            sp.dma_start(bvb[:], I["xbv"].rearrange("(o n) -> o n", o=1).to_broadcast((P, 4 * C))).then_inc(ld_ctx, 16)
            sp.dma_start(rmsw[:], I["rms"].rearrange("(o n) -> o n", o=1).to_broadcast((P, D))).then_inc(ld_f, 16)
            sp.dma_start(rw[:], I["rw"]).then_inc(ld_f, 16)

            def x_step(m, k):
                if valid(k, m, 0):
                    sp.wait_ge(x_mte, done(2 * m + 1))
                    dst = qx[MAXROW:MAXROW + 3 * XROW + 1:XROW, k % 4, 1, :].bitcast(F32)
                    sp.dma_start(dst, mrow[:, k % 2, 1, :].bitcast(F32)).then_inc(x_mrow[(k % 4) * 2 + 1], 16)
                if valid(k, m, 2):
                    sp.wait_ge(x_stack, done(2 * (m + 2) + 1))
                    sp.wait_ge(x_s2, free(8 * (m + 2) + 7, 32))
                    for j in range(4):
                        r = slice(XROW * j, XROW * j + XROW)
                        sp.dma_start(kmx[r, (k + 2) % 4, j::4, :].bitcast(F32),
                                     kstage[r, k % 2, :, :].bitcast(F32)).then_inc(x_km[(k + 2) % 4], 16)
                if valid(k, m, 1):
                    sp.wait_ge(x_mte, done(2 * (m + 1)))
                    dst = qx[MAXROW:MAXROW + 3 * XROW + 1:XROW, (k + 1) % 4, 0, :].bitcast(F32)
                    sp.dma_start(dst, mrow[:, (k + 1) % 2, 0, :].bitcast(F32)).then_inc(x_mrow[((k + 1) % 4) * 2], 16)

            def a_step(n, k):
                if n == NPAIR + 1:
                    sp.wait_ge(a_x1, done(NPAIR - 1))
                    for o, name in ((wgu, "wgu"), (wdn, "wdn")):
                        sp.dma_start(o[:], I[name]).then_inc(ld_f2, 16)


            for n in (-3, -2):
                x_step(n, n)
            a_step(NPAIR + 1, NPAIR + 1)
            x_step(-1, -1)
            steps(sp, None, x_step, 4, 0, 1, B // 4 - 1, B)

            sp.wait_ge(f_wT, done(0))
            for e in range(NE):
                sp.wait_ge(f_wb, free(e, 2))
                sp.dma_start(wrow[:, e % 2, :], wT[e:e + 1, :]).then_inc(f_wrow[e % 2], 16)
            for t in range(NPAIR):
                sp.wait_ge(f_o, done(t))
                sp.dma_start(out.rearrange("(n p) d -> p n d", p=P)[:, t, :], fy[:, t, :]).then_inc(st_out, 16)
            sp.wait_ge(st_out, 16 * NPAIR)

        @block.gpsimd
        def _(pool):
            g = nc.gpsimd
            link = Chain(pool, pool_link)
            for s in credit.values():
                pool.sem_inc(s, CREDIT)
            pool.sem_inc(credited, 1)
            g.memset(half[:, 0:1], -0.5)
            g.memset(half[:, 1:2], LN_EPS)
            g.memset(half[:, 2:3], RMS_EPS)
            g.memset(half[:, 3:4], 1.0 / D)
            g.memset(kmx[:].bitcast(F32), 0.0).then_inc(zeroed, 1)
            link(g.memset(vst[:], 0.0))
            g.memset(vst[:, :, :, :, :, XD:XD + 1], 1.0).then_inc(zeroed, 1)
            pool.wait_ge(ld_c, 32)
            pool.wait_ge(consts_ready, 1)
            pool.wait_ge(p0_act, 6)
            pool.wait_ge(p0_dve, 6)

            def rstd_of(v, eps_col, o, w):
                link(g.tensor_tensor(o, v, half[:, eps_col:eps_col + 1].to_broadcast((P, w)), ALU.add))
                return g.tensor_tensor(o, o, half[:, 0:1].to_broadcast((P, w)), ALU.pow)

            def a_step(n, k):
                if valid(k, n, 1, NPAIR):
                    u = (k + 1) % 2
                    pool.wait_ge(a_s2, free(n + 1, 2))
                    for gr in range(2):
                        g.tensor_tensor(qm[:, u, gr],
                                        QT[:, gr, bass.ds((n + 1) * P, P)].rearrange("p (o t) -> p o t", o=1).to_broadcast((P, 8, P)),
                                        K("headmask").rearrange("p (h o) -> p h o", o=1).to_broadcast((P, 8, P)),
                                        ALU.mult).then_inc(a_qm, 1)
                if valid(k, n, -2, NPAIR):
                    u = k % 2
                    pool.wait_ge(a_var, done(n - 2))
                    rstd_of(mv[:, u, 1:2], 1, rstd[:, u:u + 1], 1).then_inc(a_rstd, 1)
            a_step.links = 2
            def x_step(m, k):
                if k % 2 and valid_pair(m, k, 3):
                    n = pair_of(m, k, 3)
                    for w in range(2):
                        pool.wait_ge(x_ropes, done(2 * n + w))
                        pool.wait_ge(x_lo, free(2 * n + w, 2))
                        g.tensor_tensor(roped[:, w], rope[:, w, 0], rope[:, w, 1], ALU.add).then_inc(x_roped, 1)
                    for w in range(2):
                        pool.wait_ge(x_hi, done(2 * n + w))
                        g.tensor_tensor(hilo[:, ((k + 3) // 2) % 2, w, 1], roped[:, w], hilo[:, ((k + 3) // 2) % 2, w, 0].bitcast(F32),
                                        ALU.subtract).then_inc(x_lo, 1)
                if k % 2 and valid_pair(m, k, -3):
                    n = pair_of(m, k, -3)
                    pool.wait_ge(x_var, done(n))
                    rstd_of(mv[:, 0, 1:2], 1, rstd[:, 0:1], 1).then_inc(x_rstd, 1)
                if k % 2 and valid_pair(m, k, -3):
                    n, u = pair_of(m, k, -3), ((k - 3) // 2) % 2
                    pool.wait_ge(x_sq, done(n))
                    link(g.tensor_tensor(ms[:, u:u + 1], ms[:, u:u + 1], half[:, 3:4], ALU.mult))
                    rstd_of(ms[:, u:u + 1], 2, rr[:, u:u + 1], 1).then_inc(x_rr, 1)
            x_step.links = 2 + 4

            def split_weights(ei):
                pool.wait_ge(f_whi, done(ei))
                e = expert(ei)
                g.tensor_tensor(w_r[:, ei % 2, 1, 0:4 * F], wgu[:, e].rearrange("p u c f -> p (u c f)"),
                                w_r[:, ei % 2, 0, 0:4 * F].bitcast(F32), ALU.subtract)
                g.tensor_tensor(w_r[:, ei % 2, 1, 4 * F:WE], wdn[:, e], w_r[:, ei % 2, 0, 4 * F:WE].bitcast(F32),
                                ALU.subtract).then_inc(f_wlo, 1)

            all_steps(pool, link, a_step, x_step, lambda: None, lambda: split_weights(0))

            for ei in range(1, NE + 1):
                e = expert(ei)
                split_weights(ei)
                pool.wait_ge(f_wrow[e % 2], 16 * (e // 2 + 1))
                pool.wait_ge(f_act, free(2 * e + 3, 4))
                g.partition_broadcast(wb[:, e % 2, :], wrow[0:1, e % 2, :]).then_inc(f_wb, 1)
            for hf in range(2):
                pool.wait_ge(f_var, done(4 * hf + 3))
                t = slice(4 * hf, 4 * hf + 4)
                rstd_of(fmv[:, t, 1], 1, frstd[:, t], 4).then_inc(f_rstd, 1)

        @block.scalar
        def _(sc):
            a = nc.scalar
            link = Chain(sc, act_link)
            evac_phase0(sc, lambda o, i: a.copy(o, i), p0_act, 0)
            sc.wait_ge(p0_dve, 6)
            sc.wait_ge(p0_act, 6)
            sc.wait_ge(vbd_zero, 1)
            sc.wait_ge(credited, 1)

            def a_step(n, k):
                if valid(k, n, 1, NPAIR):
                    u, tok = (k + 1) % 2, bass.ds((n + 1) * P, P)
                    sc.wait_ge(a_s2, free(n + 1, 2))
                    a.copy(qst[:, u], QT[:, :, tok]).then_inc(a_st, 1)
                    a.copy(kst[:, u], KT[:, :, tok]).then_inc(a_st, 1)
                if valid(k, n, 0, NPAIR):
                    u = k % 2
                    sc.wait_ge(a_pv, free(n, 2))
                    for b in range(2):
                        t = slice(64 * b, 64 * b + 64)
                        last = a.copy(vbd[t, u, :, b, 0:HD], V[t, bass.ds(n, 1), :].rearrange("p o (h d) -> p (o h) d", h=H))
                    last.then_inc(a_vbd, 1)
                    sc.wait_ge(a_s2, done(n))
                    a.activation(pt[:, u].rearrange("p h q -> p (h q)"), bank[:, 2:4, :].rearrange("p a b -> p (a b)"),
                                 ACT.Exp, scale=float(HD) ** -0.5).then_inc(a_pt, 1)
                if valid(k, n, -1, NPAIR):
                    u = (k - 1) % 2
                    sc.wait_ge(a_t, done(n - 1))
                    sc.wait_ge(a_y, free(n - 1, 2))
                    a.copy(ot[:, u].rearrange("p h b q -> p b h q"),
                           bank[:, 5, 0:256].rearrange("p (b h q) -> p b h q", b=2, h=2)).then_inc(a_ot, 1)
            def evac_m(m, k, gr):
                sc.wait_ge(x_mt, done(2 * m + gr))
                wait_mrow_free(sc, m, k, gr)
                a.copy(mrow[:, k % 2, gr, :], bank[0:4, 2, 0:256]).then_inc(x_mte, 1)

            def x_step(m, k):
                for t in range(8):
                    mb, kb, tb = s2_tile(m, k, t)
                    if valid(kb, mb, 0):
                        i = 8 * mb + tb
                        sc.wait_ge(x_s2, done(i))
                        if tb % 4 == 0:
                            sc.wait_ge(x_pv, free(2 * mb + tb // 4, 2))
                        a.activation(px[:, tb // 4, tb % 4].rearrange("p c q -> p (c q)"), bank[:, 5 + t % 2, :], ACT.Exp,
                                     scale=float(XD) ** -0.5).then_inc(x_exp, 1)
                    if t == 2 and valid(k, m, 0):
                        evac_m(m, k, 1)
                    if t == 3 and valid(k, m, 2):
                        s = (k + 2) % 4
                        for w in range(2):
                            sc.wait_ge(x_spread, done(2 * (m + 2) + w))
                            if w == 0:
                                sc.wait_ge(x_s2, free(8 * (m + 2) + 7, 32))
                                a.copy(qx[:, s], bank[:, 0, :].rearrange("p (g q) -> p g q", g=2)).then_inc(x_stack, 1)
                            else:
                                wait_km_staged(sc, m, k)
                                a.activation(kstage[:, k % 2], bank[:, 1, :].rearrange("p (g q) -> p g q", g=2),
                                             ACT.Identity, bias=K("onescol")).then_inc(x_stack, 1)
                    if t == 0 and k % 2 and valid(k, m, 1):
                        n = pair_of(m, k, 1)
                        sc.wait_ge(x_v, free(n, 1))
                        a.copy(cst[:], cx[:, bass.ds(n, 1), :].rearrange("p o d -> p (o d)")).then_inc(x_cst, 1)
                    if t == 2 and k % 2 and valid_pair(m, k, 3):
                        n = pair_of(m, k, 3)
                        for w in range(2):
                            sc.wait_ge(x_roped, done(2 * n + w))
                            sc.wait_ge(x_spread, free(4 * n + 3, 8))
                            a.copy(hilo[:, ((k + 3) // 2) % 2, w, 0], roped[:, w]).then_inc(x_hi, 1)
                    if t == 6 and valid(k, m, 1):
                        evac_m(m + 1, k + 1, 0)
                    if t == 4 and k % 2 and valid_pair(m, k, -3):
                        n, u = pair_of(m, k, -3), ((k - 3) // 2) % 2
                        sc.wait_ge(x_x2, done(n))
                        if not (isinstance(n, int) and n == 0):
                            sc.wait_ge(x_sq, free(n, 1))
                        sc.wait_ge(x_rr, free(n, 2))
                        a.activation(sq[:], x_sb[:, bass.ds(n, 1), :].rearrange("p o d -> p (o d)"), ACT.Square,
                                     accum_out=ms[:, u:u + 1]).then_inc(x_sq, 1)
                    if t == 4 and k % 2 == 0 and valid_pair(m, k, -4):
                        n = pair_of(m, k, -4)
                        sc.wait_ge(x_ht, done(n))
                        a.copy(hT[:, 0, :, bass.ds(n * P, P)], bank[:, 2, 0:D].rearrange("p (c t) -> p c t", c=2)).then_inc(x_hhi, 1)

            def split_weights(ei):
                e = expert(ei)
                sc.wait_ge(f_dn, free(2 * ei + 1, 4))
                a.copy(w_r[:, ei % 2, 0, 0:4 * F], wgu[:, e].rearrange("p u c f -> p (u c f)"))
                a.copy(w_r[:, ei % 2, 0, 4 * F:WE], wdn[:, e]).then_inc(f_whi, 1)

            def x_first():
                sc.wait_ge(ld_ctx, 16 * 5)

            def f_first():
                sc.wait_ge(x_s2, done(8 * B - 1))
                sc.wait_ge(ld_f2, 32)
                split_weights(0)

            all_steps(sc, None, a_step, x_step, x_first, f_first)

            for hf in range(2):
                sc.wait_ge(f_lt, done(hf))
                a.copy(lT[:, 512 * hf:512 * hf + 512], bank[0:NE, 5 + hf, :]).then_inc(f_lte, 1)
            split_weights(1)
            sc.wait_ge(f_lsub, done(0))
            a.activation(ex[:], lg[:], ACT.Exp).then_inc(f_exp, 1)
            for i in range(NI):
                sc.wait_ge(f_gu, done(i))
                sc.wait_ge(f_prod, free(i, 2))
                a.activation(sl[:, i % 2], bank[:, GU[i % 2], :], ACT.Silu).then_inc(f_silu, 1)
                if i == 1:
                    sc.wait_ge(f_wtp, done(0))
                    a.copy(wT[:], bank[0:NE, 1:3, :].rearrange("p a b -> p (a b)")).then_inc(f_wT, 1)
                sc.wait_ge(f_act, done(i))
                sc.wait_ge(f_dn, free(i, 2))
                a.copy(act_r[:, i % 2, 0], act[:, i % 2]).then_inc(f_ahi, 1)
                if i % 2 == 0 and 2 <= i and i // 2 + 1 <= NE:
                    split_weights(i // 2 + 1)

        @block.vector
        def _(ve):
            v = nc.vector
            link = Chain(ve, dve_link)
            link(v.memset(vbd[:], 0.0))
            v.memset(vbd[0:64, :, :, 0, HD:HD + 1], 1.0)
            v.memset(vbd[64:128, :, :, 1, HD:HD + 1], 1.0).then_inc(vbd_zero, 1)
            evac_phase0(ve, lambda o, i: v.tensor_copy(o, i), p0_dve, 1)
            ve.wait_ge(ld_c, 32)
            v.tensor_copy(sel_r[:], sel[:])
            v.tensor_copy(sameb_r[:], K("sameb")).then_inc(consts_ready, 1)
            ve.wait_ge(ld_ctx, 16 * 5)
            ve.wait_ge(ld_f, 32)
            link(v.tensor_copy(rw_r[:, 0], rw[:]))
            v.tensor_tensor(rw_r[:, 1], rw[:], rw_r[:, 0].bitcast(F32), ALU.subtract).then_inc(rw_ready, 1)
            for n in (1, 3):
                link(v.tensor_tensor(xw[:, n], xw[:, n], K("signrow"), ALU.mult))
                link(v.tensor_tensor(xb[:, n:n + 1], xb[:, n:n + 1], K("signcol"), ALU.mult))
            ve.wait_ge(p0_act, 6)
            ve.wait_ge(p0_dve, 6)
            ve.wait_ge(credited, 1)
            ve.wait_ge(ld_xn, 32)

            def statistics(src, u, sem_var, bn_n):
                v.bn_stats(stats[:, u], src).then_inc(bn_done, 1)
                ve.wait_ge(bn_done, done(bn_n))
                v.memset(wait_here[:], 0.0)
                v.bn_aggr(mv[:, u], stats[:, u]).then_inc(sem_var, 1)

            def normalised(o, src, u, sem_rstd, n):
                ve.wait_ge(sem_rstd, done(n))
                return v.tensor_scalar(o, src, mv[:, u, 0:1], rstd[:, u:u + 1], ALU.subtract, ALU.mult)

            def a_step(n, k):
                if valid(k, n, 0, NPAIR):
                    u = k % 2
                    ve.wait_ge(a_s1, done(n))
                    link(v.tensor_reduce(negmax[:, u], bank[:, 0:2, :].rearrange("p a (h k) -> p (a h) k", k=C), AX.X, ALU.max,
                                         negate=True))
                    ve.wait_ge(a_s2, free(n, 2))
                    v.tensor_tensor(shift[:, u], K("fold").rearrange("p (o q) -> p o q", o=1).to_broadcast((P, H, C)),
                                    negmax[:, u].rearrange("p (h o) -> p h o", o=1).to_broadcast((P, H, C)),
                                    ALU.mult).then_inc(a_shift, 1)
                if valid(k, n, -2, NPAIR):
                    u = k % 2
                    ve.wait_ge(a_y, done(n - 2))
                    v.tensor_tensor(ysum[:, u], bank[:, 6 + u, 0:D], x_sb[:, bass.ds(n - 2, 1), :].rearrange("p o d -> p (o d)"),
                                    ALU.add).then_inc(a_sum, 1)
                    ve.wait_ge(a_sum, done(n - 2))
                    statistics(ysum[:, u], u, a_var, n - 2)
                if valid(k, n, -1, NPAIR):
                    u = (k - 1) % 2
                    ve.wait_ge(a_pv, done(n - 1))
                    o = bank[:, 4, 0:8 * 2 * (HD + 1)].rearrange("p (h b d) -> p h b d", h=8, b=2)
                    link(v.reciprocal(rsum[:, u], o[:, :, :, HD]))
                    ve.wait_ge(a_t, free(n - 1, 2))
                    for b in range(2):
                        last = v.tensor_tensor(on[:, u, b], o[:, :, b, 0:HD],
                                               rsum[:, u, :, b:b + 1].to_broadcast((P, 8, HD)), ALU.mult)
                    last.then_inc(a_on, 1)
                if valid(k, n, 1, NPAIR):
                    u = (k + 1) % 2
                    ve.wait_ge(a_s1, free(n + 1, 2))
                    for gr in range(2):
                        v.tensor_tensor(km[:, u, gr],
                                        KT[:, gr, bass.ds((n + 1) * P, P)].rearrange("p (o t) -> p o t", o=1).to_broadcast((P, 8, P)),
                                        K("headmask").rearrange("p (h o) -> p h o", o=1).to_broadcast((P, 8, P)),
                                        ALU.mult).then_inc(a_km, 1)
                if valid(k, n, -2, NPAIR):
                    u = k % 2
                    normalised(x_sb[:, bass.ds(n - 2, 1), :].rearrange("p o d -> p (o d)"), ysum[:, u], u, a_rstd,
                               n - 2).then_inc(a_x1, 1)
            a_step.links = 4
            def x_step(m, k):
                for t in range(8):
                    if valid(k, m, 1):
                        ve.wait_ge(x_s1, done(8 * (m + 1) + t))
                        if t % 4 == 0:
                            ve.wait_ge(x_mt, free(2 * (m + 1) + t // 4, 4))
                        v.tensor_reduce(nmax[:, (k + 1) % 2, t // 4, (t // 2) % 2, 2 * (t % 2):2 * (t % 2) + 2],
                                        bank[:, 3 + t % 2, :].rearrange("p (h k) -> p h k", h=2), AX.X, ALU.max,
                                        negate=True).then_inc(x_max, 1)
                    s = (k - 1) % 2
                    if t == 4 and valid(k, m, -1):
                        ve.wait_ge(x_pv, done(2 * (m - 1) + 1))
                        v.transpose(tn[:, s].rearrange("p a b -> p (a b)"), bank[:, 7, :]).then_inc(x_n1, 1)
                    if t == 5 and valid(k, m, -1):
                        ve.wait_ge(x_n1, done(m - 1))
                        link(v.reciprocal(rs[:, s], tn[:, s, :, XD]))
                        v.tensor_tensor(tn[:, s, :, 0:XD], tn[:, s, :, 0:XD],
                                        rs[:, s].rearrange("p (a o) -> p a o", o=1).to_broadcast((P, 16, XD)), ALU.mult).then_inc(x_n2, 1)
                    if t == 6 and valid(k, m, -1):
                        ve.wait_ge(x_n2, done(m - 1))
                        v.transpose(onx[:, (k - 1) % 4].rearrange("p g q -> p (g q)"),
                                    tn[:, s].rearrange("p a b -> p (a b)")).then_inc(x_norm, 1)
                    if (t == 7 and k % 2 == 0 and valid_pair(m, k, 4)) or (t == 0 and k % 2 and valid_pair(m, k, 3)):
                        n = pair_of(m, k, 4 if t == 7 else 3)
                        for w in (0 if t == 7 else 1,):
                            ve.wait_ge((x_pq, x_pk)[w], done(n))
                            ve.wait_ge(x_roped, free(2 * n + w, 2))
                            for r in range(2):
                                last = v.scalar_tensor_tensor(rope[:, w, r], bank[:, w, 256 * r:256 * r + 256],
                                                              xb[:, 2 * w + r:2 * w + r + 1], K(("cos", "sin")[r]), ALU.add, ALU.mult)
                            last.then_inc(x_ropes, 1)
                    if t == 5 and k % 2 and valid(k, m, 1):
                        n = pair_of(m, k, 1)
                        ve.wait_ge(x_v, done(n))
                        ve.wait_ge(x_pv, free(4 * n + 3, 8))
                        v.tensor_tensor(vst[:, ((k + 1) // 2) % 2].rearrange("p c b h r -> p (c b h) r")[:, :, 0:XD],
                                        bank[:, 2, 0:D].rearrange("p (n d) -> p n d", d=XD),
                                        bvb[:].rearrange("p (n d) -> p n d", d=XD), ALU.add).then_inc(x_vst, 1)
                    if t == 1 and k % 2 and valid_pair(m, k, -3):
                        n = pair_of(m, k, -3)
                        ve.wait_ge(x_y, done(n))
                        xs = x_sb[:, bass.ds(n, 1), :].rearrange("p o d -> p (o d)")
                        v.scalar_tensor_tensor(ysum[:, 0], bank[:, 2, 0:D], xb[:, 4:5], xs, ALU.add, ALU.add).then_inc(x_ysum, 1)
                        ve.wait_ge(x_ysum, done(n))
                        statistics(ysum[:, 0], 0, x_var, NPAIR + n)
                    if t == 5 and k % 2 == 0 and valid_pair(m, k, -4):
                        n = pair_of(m, k, -4)
                        ve.wait_ge(x_hhi, done(n))
                        tok = bass.ds(n * P, P)
                        v.tensor_tensor(hT[:, 1, :, tok], bank[:, 2, 0:D].rearrange("p (c t) -> p c t", c=2),
                                        hT[:, 0, :, tok].bitcast(F32), ALU.subtract).then_inc(x_hlo, 1)
                    if t == 7 and k % 2 and valid_pair(m, k, -3):
                        n, u = pair_of(m, k, -3), ((k - 3) // 2) % 2
                        ve.wait_ge(x_rr, done(n))
                        ve.wait_ge(x_ht, free(n, 2))
                        v.scalar_tensor_tensor(hx[:, u], x_sb[:, bass.ds(n, 1), :].rearrange("p o d -> p (o d)"), rr[:, u:u + 1],
                                               rmsw[:], ALU.mult, ALU.mult).then_inc(x_h, 1)
                    if t == 3 and k % 2 and valid_pair(m, k, -3):
                        n = pair_of(m, k, -3)
                        normalised(x_sb[:, bass.ds(n, 1), :].rearrange("p o d -> p (o d)"), ysum[:, 0], 0, x_rstd, n).then_inc(x_x2, 1)
            x_step.links = 4

            def x_first():
                ve.wait_ge(zeroed, 2)
                ve.wait_ge(ld_f, 32)

            all_steps(ve, link, a_step, x_step, x_first, lambda: None)

            ve.wait_ge(f_lg, done(0))
            lps = bank[:, 0, 0:NPAIR * NE].rearrange("p (t e) -> p t e", e=NE)
            link(v.tensor_reduce(lmax[:], lps, AX.X, ALU.max))
            link(v.tensor_tensor(lg[:], lps, lmax[:].rearrange("p (t o) -> p t o", o=1).to_broadcast((P, NPAIR, NE)), ALU.subtract))
            self_l = [lg[:, t].rearrange("p (i o) -> p i o", o=1).to_broadcast((P, NE, NE)) for t in range(NPAIR)]
            other_l = [lg[:, t].rearrange("p (o j) -> p o j", o=1).to_broadcast((P, NE, NE)) for t in range(NPAIR)]
            for t in range(NPAIR):
                v.tensor_tensor(gt[:, t], other_l[t], self_l[t], ALU.is_gt)
                last = v.tensor_tensor(eq[:, t], other_l[t], self_l[t], ALU.is_equal)
            last.then_inc(f_lsub, 1)
            ve.wait_ge(f_lsub, done(0))
            before = K("before").rearrange("p (o n) -> p o n", o=1).to_broadcast((P, NPAIR, NE * NE))
            link(v.tensor_tensor(eq[:].rearrange("p t i j -> p t (i j)"), eq[:].rearrange("p t i j -> p t (i j)"), before, ALU.mult))
            link(v.tensor_tensor(gt[:], gt[:], eq[:], ALU.add))
            link(v.tensor_reduce(rank[:], gt[:], AX.X, ALU.add))
            ve.wait_ge(f_exp, done(0))
            link(v.scalar_tensor_tensor(wsel[:], rank[:], 2.0, ex[:], ALU.is_lt, ALU.mult))
            link(v.tensor_reduce(wsum[:], wsel[:], AX.X, ALU.add))
            link(v.reciprocal(lmax[:], wsum[:]))
            v.tensor_tensor(wsel[:], wsel[:], lmax[:].rearrange("p (t o) -> p t o", o=1).to_broadcast((P, NPAIR, NE)),
                            ALU.mult).then_inc(f_w, 1)
            for i in range(NI):
                e, hf = order(i)
                ve.wait_ge(f_silu, done(i))
                ve.wait_ge(f_alo, free(i, 2))
                dst = act[:, i % 2] if e == NE else pr[:, i % 2]
                prod = v.tensor_tensor(dst, bank[:, GU[i % 2] + 1, :], sl[:, i % 2], ALU.mult)
                prod.then_inc(f_prod, 1)
                ve.wait_ge(f_prod, done(i))
                if e == NE:
                    ve.sem_inc(f_act, 1)
                else:
                    ve.wait_ge(f_wb, done(e))
                    v.tensor_tensor(act[:, i % 2], pr[:, i % 2], wb[:, e % 2, 512 * hf:512 * hf + 512], ALU.mult).then_inc(f_act, 1)
                ve.wait_ge(f_ahi, done(i))
                v.tensor_tensor(act_r[:, i % 2, 1], act[:, i % 2], act_r[:, i % 2, 0].bitcast(F32), ALU.subtract).then_inc(f_alo, 1)
            for hf in range(2):
                ve.wait_ge(f_dn, done(2 * NE + hf))
                for t in range(4 * hf, 4 * hf + 4):
                    link(v.tensor_tensor(fy[:, t], bank[:, ACC[t // 2], 256 * (t % 2):256 * (t % 2) + 256], x_sb[:, t], ALU.add))
                    link(v.bn_stats(fstats[:, t], fy[:, t]))
                    v.bn_aggr(fmv[:, t], fstats[:, t]).then_inc(f_var, 1)
                ve.wait_ge(f_rstd, done(hf))
                for t in range(4 * hf, 4 * hf + 4):
                    v.tensor_scalar(fy[:, t], fy[:, t], fmv[:, t, 0:1], frstd[:, t:t + 1], ALU.subtract, ALU.mult).then_inc(f_o, 1)

        @block.tensor
        def _(pe):
            mm = nc.tensor.matmul
            pe.wait_ge(ld_w, 16)
            pe.wait_ge(ld_x, 32)
            for n in range(12):
                if n >= 8:
                    pe.wait_ge((p0_act, p0_dve)[n % 2], (n - 8) // 2 + 1)
                for part in range(1 if n < 8 else 2):
                    for c in range(2):
                        if n < 8:
                            w, gr, hf = n // 4, (n // 2) % 2, n % 2
                            last = mm(bank[:, n, :], wqkv[:, w, c, P * gr:P * gr + P], xT[:, c, 512 * hf:512 * hf + 512],
                                      start=c == 0, stop=c == 1)
                        else:
                            t = 2 * (n - 8) + part
                            last = mm(bank[:, n % 8, D * part:D * part + D], xT[:, c, P * t:P * t + P], wqkv[:, 2, c, :],
                                      start=c == 0, stop=c == 1)
                last.then_inc(p0_mm, 1)
            pe.wait_ge(p0_act, 6)
            pe.wait_ge(p0_dve, 6)
            pe.wait_ge(consts_ready, 1)
            pe.wait_ge(credited, 1)
            pe.wait_ge(ld_xn, 32)

            def a_step(n, k):
                u = k % 2
                if valid(k, n, 0, NPAIR):
                    pe.wait_ge(a_st, done(2 * n + 1))
                    pe.wait_ge(a_km, done(2 * n + 1))
                    pe.wait_ge(a_shift, free(n, 1))
                    for gr in range(2):
                        for b in range(2):
                            t = slice(64 * b, 64 * b + 64)
                            last = mm(bank[t, gr, :], qst[:, u, gr, t], km[:, u, gr, :, t], start=True, stop=True)
                    last.then_inc(a_s1, 1)
                if valid(k, n, -2, NPAIR):
                    pe.wait_ge(a_ot, done(n - 2))
                    pe.wait_ge(a_x1, free(n - 2, 2))
                    for h2 in range(2):
                        last = mm(bank[:, 6 + u, 0:D], ot[:, u, h2].rearrange("p b q -> p (b q)"), wo[:, h2, :], start=h2 == 0, stop=h2 == 1)
                    last.then_inc(a_y, 1)
                if valid(k, n, -1, NPAIR):
                    w = (k - 1) % 2
                    pe.wait_ge(a_pt, done(n - 1))
                    pe.wait_ge(a_vbd, done(n - 1))
                    pe.wait_ge(a_on, free(n - 1, 1))
                    for h in range(H):
                        o = 34 * (h // 2)
                        last = mm(bank[64 * (h % 2):64 * (h % 2) + 64, 4, o:o + 34], pt[:, w, h, :],
                                  vbd[:, w, h].rearrange("p b d -> p (b d)"), start=True, stop=True, skip_group_check=True)
                    last.then_inc(a_pv, 1)
                if valid(k, n, 0, NPAIR):
                    pe.wait_ge(a_shift, done(n))
                    pe.wait_ge(a_qm, done(2 * n + 1))
                    pe.wait_ge(a_pt, free(n, 1))
                    for gr in range(2):
                        mm(bank[:, 2 + gr, :], sameb_r[:], shift[:, u, 8 * gr:8 * gr + 8, :], start=True, stop=False, skip_group_check=True)
                        for b in range(2):
                            t = slice(64 * b, 64 * b + 64)
                            last = mm(bank[t, 2 + gr, :], kst[:, u, gr, t], qm[:, u, gr, :, t], start=False, stop=True,
                                      skip_group_check=True)
                    last.then_inc(a_s2, 1)
                if valid(k, n, -1, NPAIR):
                    w = (k - 1) % 2
                    pe.wait_ge(a_on, done(n - 1))
                    pe.wait_ge(a_ot, free(n - 1, 1))
                    for b in range(2):
                        last = nc.tensor.transpose(bank[:, 5, P * b:P * b + P], on[:, w, b].rearrange("p h d -> p (h d)"), K("ident"))
                    last.then_inc(a_t, 1)

            def maxima_rows(m, k, gr):
                pe.wait_ge(x_max, done(8 * m + 4 * gr + 3))
                pe.wait_ge(x_mte, free(2 * m + gr, 1))
                if gr == 1 and k % 2 and valid_pair(m, k, -3):
                    pe.wait_ge(x_ysum, done(pair_of(m, k, -3)))
                if gr == 0 and k % 2 == 0:
                    pe.wait_ge(x_vst, done(pair_of(m, k, 0)))
                if gr == 0 and k % 2 and valid_pair(m, k, -5):
                    pe.wait_ge(x_hlo, done(pair_of(m, k, -5)))
                for c in range(2):
                    last = nc.tensor.transpose(bank[0:4, 2, P * c:P * c + P], nmax[:, k % 2, gr, c, :], K("ident"))
                last.then_inc(x_mt, 1)

            def weighted_values(m, k, gr):
                pe.wait_ge(x_exp, done(8 * m + 4 * gr + 3))
                if gr == 0:
                    pe.wait_ge(x_vst, done(pair_floor(m, k)))
                    pe.wait_ge(x_n1, free(m, 1))
                for c in range(2):
                    for j in range(4):
                        last = mm(bank[XROW * j:XROW * j + XROW, 7, D * gr:D * gr + D], vst[:, (k // 2) % 2, c, k % 2, 4 * gr + j, :],
                                  px[:, gr, j, c, :], start=c == 0, stop=c == 1, skip_group_check=True)
                last.then_inc(x_pv, 1)

            def project(m, k, w):
                n = pair_of(m, k, 4)
                if w == 0 and isinstance(m, int) and m < 0:
                    pe.wait_ge(a_x1, done(n))
                pe.wait_ge(x_stack, free(4 * n + w - 2, 2))
                src = (x_sb, cx)[w][:, bass.ds(n, 1), :].rearrange("p o d -> p (o d)")
                for r in range(2):
                    last = mm(bank[:, w, D * r:D * r + D], xw[:, 2 * w + r, :], src, start=True, stop=True,
                              skip_group_check=True)
                last.then_inc((x_pq, x_pk)[w], 1)

            def x_step(m, k):
                for t in range(8):
                    if valid(k, m, 1):
                        m1, s = m + 1, (k + 1) % 4
                        gr, c, hp = t // 4, (t // 2) % 2, t % 2
                        if t == 0:
                            pe.wait_ge(x_stack, done(2 * m1))
                            wait_km(pe, m1, k + 1)
                        pe.wait_ge(x_max, free(8 * m1 + t, 2))
                        mm(bank[:, 3 + t % 2, :], qx[:, s, gr, P * c:P * c + P],
                           kmx[:, s, 4 * gr + 2 * hp:4 * gr + 2 * hp + 2, :].rearrange("p h k -> p (h k)"),
                           start=True, stop=True).then_inc(x_s1, 1)
                    mb, kb, tb = s2_tile(m, k, t)
                    if valid(kb, mb, 0):
                        s, gr = kb % 4, tb // 4
                        if tb % 4 == 0:
                            wait_mrow(pe, mb, kb, gr)
                        pe.wait_ge(x_exp, free(8 * mb + tb, 2))
                        for c in range(2):
                            last = mm(bank[:, 5 + t % 2, D * c:D * c + D], kmx[:, s, tb, P * c:P * c + P], qx[:, s, gr, :],
                                      start=True, stop=True, skip_group_check=True)
                        last.then_inc(x_s2, 1)
                    if t == 0 and k % 2 and valid_pair(m, k, -3):
                        n = pair_of(m, k, -3)
                        pe.wait_ge(x_norm, done(2 * n + 1))
                        if valid(k, m, 0):
                            pe.wait_ge(x_mte, done(2 * m))
                        else:
                            pe.wait_ge(x_hlo, done(pair_of(m, k, -5)))
                        for gr in range(2):
                            for b in range(2):
                                last = mm(bank[64 * b:64 * b + 64, 2, 0:D], xwo[:, gr, :], onx[:, (k - 3 + b) % 4, gr, :],
                                          start=gr == 0, stop=gr == 1, skip_group_check=True)
                        last.then_inc(x_y, 1)
                    if t == 2 and valid(k, m, 0):
                        maxima_rows(m, k, 1)
                    if t == 2 and valid(k, m, 2):
                        n = pair_floor2(m, k)
                        b = k % 2
                        sl_ = ((k + 2) // 2) % 2
                        for w in range(2):
                            pe.wait_ge(x_lo, done(2 * n + w))
                            pe.wait_ge(x_stack, free(2 * (m + 2) + w, 2))
                            if k % 2 and valid(k, m, 3):
                                pe.wait_ge(x_ropes, done(2 * pair_of(m, k, 3) + w))
                            for gr in range(2):
                                for part in range(2):
                                    last = mm(bank[:, w, D * gr:D * gr + D], sel_r[:, ((w * 2 + b) * 2 + gr) * 2 + part, :],
                                              hilo[:, sl_, w, part, :], start=part == 0, stop=part == 1, skip_group_check=True)
                            last.then_inc(x_spread, 1)
                    if t == 4 and k % 2 == 0 and valid_pair(m, k, -4):
                        n, u = pair_of(m, k, -4), ((k - 4) // 2) % 2
                        pe.wait_ge(x_h, done(n))
                        if valid(k, m, 0):
                            pe.wait_ge(x_mte, done(2 * m + 1))
                        for c in range(2):
                            last = nc.tensor.transpose(bank[:, 2, P * c:P * c + P], hx[:, u, P * c:P * c + P], K("ident"))
                        last.then_inc(x_ht, 1)
                    if t == 3 and valid(k, m, -1):
                        weighted_values(m - 1, k - 1, 1)
                    if t == 4 and k % 2 and valid(k, m, 1):
                        n = pair_of(m, k, 1)
                        pe.wait_ge(x_cst, done(n))
                        if valid(k, m, 0):
                            pe.wait_ge(x_mte, done(2 * m + 1))
                        for c in range(2):
                            last = mm(bank[:, 2, P * c:P * c + P], cst[:, P * c:P * c + P], xw[:, 4, :], start=True, stop=True,
                                      skip_group_check=True)
                        last.then_inc(x_v, 1)
                    if t == 6 and valid(k, m, 1):
                        maxima_rows(m + 1, k + 1, 0)
                    if t in (5, 6) and k % 2 == 0 and valid(k, m, 4):
                        project(m, k, t - 5)
                    if t == 7 and valid(k, m, 0):
                        weighted_values(m, k, 0)

            def gate_up(i):
                hf = i % 2
                pe.wait_ge(f_wlo, done(i // 2))
                pe.wait_ge(f_prod, free(i, 2))
                t = slice(512 * hf, 512 * hf + 512)
                for u in range(2):
                    n = 0
                    for c in range(2):
                        for wp, hp in ((0, 0), (0, 1), (1, 0)):
                            last = mm(bank[:, GU[i % 2] + u, :], w_r[:, (i // 2) % 2, wp, (2 * u + c) * F:(2 * u + c) * F + F],
                                      hT[:, hp, c, t], start=n == 0, stop=n == 5)
                            n += 1
                last.then_inc(f_gu, 1)

            def x_first():
                pe.wait_ge(ld_ctx, 16 * 5)
                pe.wait_ge(zeroed, 2)
                pe.wait_ge(a_shift, done(NPAIR - 1))
                pe.wait_ge(a_pt, done(NPAIR - 1))

            def f_first():
                pe.wait_ge(x_hlo, done(3))
                gate_up(0)

            all_steps(pe, None, a_step, x_step, x_first, f_first)

            pe.wait_ge(x_hlo, done(NPAIR - 1))
            pe.wait_ge(rw_ready, 1)
            for hf in range(2):
                n = 0
                for c in range(2):
                    for wp, hp in ((0, 0), (0, 1), (1, 0)):
                        last = mm(bank[:, 5 + hf, :], rw_r[:, wp, c, :], hT[:, hp, c, 512 * hf:512 * hf + 512], start=n == 0, stop=n == 5)
                        n += 1
                last.then_inc(f_lt, 1)
            pe.wait_ge(f_lte, done(1))
            for t in range(NPAIR):
                last = nc.tensor.transpose(bank[:, 0, NE * t:NE * t + NE], lT[:, P * t:P * t + P], K("ident")[0:NE, 0:NE])
            last.then_inc(f_lg, 1)

            def down(i):
                e, hf = order(i)
                pe.wait_ge(f_alo, done(i))
                for t in range(4):
                    tt = 4 * hf + t
                    for n, (ap, wp) in enumerate(((0, 0), (0, 1), (1, 0))):
                        last = mm(bank[:, ACC[tt // 2], D * (tt % 2):D * (tt % 2) + D], act_r[:, i % 2, ap, P * t:P * t + P],
                                  w_r[:, (i // 2) % 2, wp, 4 * F:WE], start=(i < 2 and tt % 2 == 0 and n == 0),
                                  stop=(i >= 2 * NE and n == 2), skip_group_check=True)
                last.then_inc(f_dn, 1)

            gate_up(1)
            pe.wait_ge(f_w, done(0))
            for t in range(NPAIR):
                last = nc.tensor.transpose(bank[0:NE, 1 + t // 4, P * (t % 4):P * (t % 4) + P], wsel[:, t, :], K("ident"))
            last.then_inc(f_wtp, 1)
            pe.wait_ge(f_wT, done(0))
            for i in range(NI):
                down(i)
                if i + 2 < NI:
                    gate_up(i + 2)


def kernel(**inp):
    import concourse.bacc as bacc
    from concourse.bass_utils import run_bass_kernel_spmd

    def arr(a):
        return np.ascontiguousarray(np.asarray(a))

    a = {k: arr(v) for k, v in inp.items()}
    partner = np.arange(C) ^ (XD // 2)
    evenodd = np.concatenate([np.arange(HD) + HD * h for h in list(range(0, H, 2)) + list(range(1, H, 2))])
    x2d = a["x"].reshape(NTOK, D)
    chunks = lambda w: w.reshape(2, P, -1).transpose(1, 0, 2)

    def twice(w):
        z = np.zeros((P, P), w.dtype)
        z[:C, :C] = z[C:, C:] = w
        return z

    def spread(w):
        z = np.zeros((P, 2, C), w.dtype)
        for h in range(XH):
            r = XROW * (h % 4)
            z[r:r + XD, h // 4] = w[XD * h:XD * h + XD]
        return z

    qT, kT, vT, oT = (a["L0_xattn_W" + n].T for n in "qkvo")
    bq, bk, bo = (a["L0_xattn_b" + n] for n in "qko")
    gate = np.concatenate([a["L0_ffn_w_gate"], a["L0_ffn_sw_gate"][None]])
    up = np.concatenate([a["L0_ffn_w_up"], a["L0_ffn_sw_up"][None]])
    down = np.concatenate([a["L0_ffn_w_down"], a["L0_ffn_sw_down"][None]])
    A = {
        "x": x2d, "xT": x2d.T, "ctx": a["ctx_2048"].reshape(NTOK, D),
        "wqkv": np.stack([chunks(a["L0_attn_W" + n].T) for n in "qkv"], axis=1),
        "wo": chunks(a["L0_attn_Wo"].T[evenodd]),
        "xw": np.stack([twice(w) for w in (qT, qT[:, partner], kT, kT[:, partner], vT)], axis=1),
        "xwo": spread(oT),
        "xb": np.stack([np.tile(w, 2) for w in (bq, bq[partner], bk, bk[partner], bo)], axis=1),
        "xbv": np.tile(a["L0_xattn_bv"], 4), "rms": a["L0_ffn_rms_weight"],
        "wgu": np.stack([gate, up], axis=1).reshape(NE + 1, 2, 2, P, F).transpose(3, 0, 1, 2, 4),
        "wdn": down.transpose(1, 0, 2),
        "rw": np.concatenate([chunks(a["L0_ffn_router_w"]), np.zeros((P, 2, P - NE), np.float32)], axis=2),
        "con": constant_block()[0], "sel": constant_block()[2],
    }
    nc = bacc.Bacc("TRN2", target_bir_lowering=False, num_devices=1)
    arrays, aps = {}, {}
    for name, v in A.items():
        v = np.ascontiguousarray(v)
        arrays["in_" + name] = v
        aps[name] = nc.dram_tensor("in_" + name, v.shape, mybir.dt.from_np(v.dtype), kind="ExternalInput").ap()
    out = nc.dram_tensor("out_y", (NTOK, D), F32, kind="ExternalOutput").ap()
    build(nc, aps, out)
    r = run_bass_kernel_spmd(nc, [arrays], core_ids=[0])
    return r.results[0]["out_y"].reshape(B, C, D)
```

```python
from contextlib import ExitStack

import numpy as np
import concourse.bass as bass
from concourse import mybir

F32 = mybir.dt.float32
F32R = mybir.dt.float32r
ALU = mybir.AluOpType
ACT = mybir.ActivationFunctionType
AX = mybir.AxisListType

P = 128
B, C, D = 16, 64, 256
NTOK = B * C
NPAIR = B // 2
H, HD = 16, 16
XH, XD = 8, 8
NE, F = 8, 128
LN_EPS, RMS_EPS = 1e-5, 1e-6
XROW = 32
MAXROW = 24
CREDIT = 32


def done(n):
    return n + 1 + CREDIT


def free(n, depth):
    return n + 1 + CREDIT - depth


def constant_block():
    p = np.arange(P)
    blocks = {}
    blocks["ident"] = np.eye(P)
    inv = (np.float32(1.0) / np.power(np.float32(10000.0), np.arange(0, XD, 2, dtype=np.float32) / np.float32(XD))).astype(np.float32)
    ang = (np.arange(D, dtype=np.float32)[:, None] * inv[None, :]).astype(np.float32)
    ang = np.concatenate([ang, ang], axis=1)
    blocks["cos"] = np.cos(ang).T[p % XD]
    blocks["sin"] = np.sin(ang).T[p % XD]
    blocks["signrow"] = np.broadcast_to(np.where(p % XD < XD // 2, -1.0, 1.0), (P, P))
    blocks["signcol"] = np.where(p % XD < XD // 2, -1.0, 1.0)[:, None]
    blocks["headmask"] = (p[:, None] // HD == np.arange(8)[None, :])
    blocks["fold"] = (p[:, None] % C == np.arange(C)[None, :])
    blocks["sameb"] = (p[:, None] // C == p[None, :] // C)
    blocks["onescol"] = (p % XROW == MAXROW)[:, None]
    sel = np.zeros((P, 2, 2, 2, 2, P))
    for w, parts in enumerate(((0, 0, 1), (0, 1, 0))):
        for b in range(2):
            for h in range(XH):
                for c, part in enumerate(parts):
                    for d in range(XD):
                        sel[64 * b + XD * h + d, w, b, h // 4, part, XROW * (h % 4) + XD * c + d] = 1
    at, cols = {}, 0
    for k, v in blocks.items():
        at[k] = (cols, cols + v.shape[1])
        cols += v.shape[1]
    return np.concatenate([np.asarray(v, np.float32) for v in blocks.values()], axis=1), at, sel.reshape(P, -1).astype(np.float32)


def build(nc, I, out):
    _, CAT, _ = constant_block()
    ncon = max(v[1] for v in CAT.values())
    ctx = ExitStack()
    with ctx:
        def sb(name, shape, dt=F32):
            return ctx.enter_context(nc.sbuf_tensor("b_" + name, shape, dt))

        def sem(name):
            return ctx.enter_context(nc.semaphore(name))

        bank = ctx.enter_context(nc.psum_tensor("bank", [P, 8, 512], F32))
        con = sb("con", [P, ncon])
        K = lambda k: con[:, CAT[k][0]:CAT[k][1]]
        x_sb = sb("x", [P, NPAIR, D])
        sel_r = sb("sel_r", [P, 16, P], F32R)
        sameb_r = sb("sameb_r", [P, P], F32R)
        cx = sb("cx", [P, NPAIR, D])
        xw = sb("xw", [P, 5, P])
        xwo = sb("xwo", [P, 2, C])
        xb = sb("xb", [P, 5])
        bvb = sb("bvb", [P, 4 * C])
        rmsw = sb("rmsw", [P, D])
        rw = sb("rw", [P, 2, P])
        rw_r = sb("rw_r", [P, 2, 2, P], F32R)
        ysum = sb("ysum", [P, 2, D])
        stats = sb("stats", [P, 2, 6])
        mv = sb("mv", [P, 2, 2])
        rstd = sb("rstd", [P, 2])
        wait_here = sb("wait_here", [P, 1])
        half = sb("half", [P, 4])
        kmx = sb("kmx", [P, 4, XH, D], F32R)
        qx = sb("qx", [P, 4, 2, D], F32R)
        kstage = sb("kstage", [P, 2, 2, D], F32R)
        rope = sb("rope", [P, 2, 2, D])
        roped = sb("roped", [P, 2, D])
        hilo = sb("hilo", [P, 2, 2, 2, D], F32R)
        cst = sb("cst", [P, D])
        vst = sb("vst", [P, 2, 2, 2, XH, XROW])
        nmax = sb("nmax", [P, 2, 2, 2, 4])
        mrow = sb("mrow", [4, 2, 2, D], F32R)

        ld_x, ld_w = [sem("ld_x0"), sem("ld_x1")], [sem("ld_wq"), sem("ld_wkv")]
        ld_xn, ld_c, ld_f = sem("ld_xn"), sem("ld_c"), sem("ld_f")
        ld_ctx, ld_f2 = sem("ld_ctx"), sem("ld_f2")
        zeroed = sem("zeroed")
        vbd_zero = sem("vbd_zero")
        consts_ready = sem("consts_ready")
        p0_mm, p0_act, p0_dve = sem("p0_mm"), sem("p0_act"), sem("p0_dve")
        credit = {}

        def dsem(name):
            credit[name] = sem(name)
            return credit[name]

        dve_link, pool_link = sem("dve_link"), sem("pool_link")
        a_st, a_km, a_qm, a_vbd = dsem("a_st"), [dsem("a_km0"), dsem("a_km1")], dsem("a_qm"), dsem("a_vbd")
        a_s1, a_max, a_shift, a_s2, a_pt, a_pv = dsem("a_s1"), dsem("a_max"), dsem("a_shift"), dsem("a_s2"), dsem("a_pt"), dsem("a_pv")
        a_s2_first, a_pt_first = dsem("a_s2_first"), dsem("a_pt_first")
        a_on, a_t, a_ot, a_y = dsem("a_on"), dsem("a_t"), dsem("a_ot"), dsem("a_y")
        bn_done = dsem("bn_done")
        a_var, a_rstd, a_x1, a_sum = dsem("a_var"), dsem("a_rstd"), dsem("a_x1"), dsem("a_sum")
        x_pq, x_pk, x_ropes, x_roped, x_hi, x_lo = (dsem("x_pq"), dsem("x_pk"), dsem("x_ropes"), dsem("x_roped"),
                                                    dsem("x_hi"), dsem("x_lo"))
        x_spread = [dsem("x_spread_q"), dsem("x_spread_k")]
        x_stack = [dsem("x_stack_q"), dsem("x_stack_k")]
        x_cst, x_v, x_vst = dsem("x_cst"), dsem("x_v"), dsem("x_vst")
        x_km = [[sem(f"x_km{s}_{hp}") for hp in range(2)] for s in range(4)]
        x_mrow = [sem(f"x_mrow{s}") for s in range(8)]
        x_s1, x_max, x_mt, x_mte = dsem("x_s1"), dsem("x_max"), dsem("x_mt"), dsem("x_mte")
        x_s2, x_exp, x_pv, x_norm = dsem("x_s2"), dsem("x_exp"), dsem("x_pv"), dsem("x_norm")
        x_n1, x_n2 = dsem("x_n1"), dsem("x_n2")
        x_y, x_ysum, x_var, x_rstd, x_x2 = dsem("x_y"), dsem("x_ysum"), dsem("x_var"), dsem("x_rstd"), dsem("x_x2")
        x_sq, x_rr, x_h, x_ht, x_hhi, x_hlo = dsem("x_sq"), dsem("x_rr"), dsem("x_h"), dsem("x_ht"), dsem("x_hhi"), dsem("x_hlo")
        f_lt, f_lte, f_lg, f_lsub, f_exp, f_w = dsem("f_lt"), dsem("f_lte"), dsem("f_lg"), dsem("f_lsub"), dsem("f_exp"), dsem("f_w")
        f_wtp, f_wT, f_wb = dsem("f_wtp"), dsem("f_wT"), dsem("f_wb")
        f_wrow = [sem("f_wrow0"), sem("f_wrow1")]
        f_whi, f_wlo, f_ahi, f_alo = dsem("f_whi"), dsem("f_wlo"), dsem("f_ahi"), dsem("f_alo")
        f_gu, f_silu, f_prod, f_act, f_dn = [dsem("f_gu0"), dsem("f_gu1")], dsem("f_silu"), dsem("f_prod"), dsem("f_act"), dsem("f_dn")
        f_sum, f_var, f_rstd, f_o, st_out = dsem("f_sum"), dsem("f_var"), dsem("f_rstd"), dsem("f_o"), sem("st_out")
        rw_ready = sem("rw_ready")
        x_consts = sem("x_consts")
        credited = sem("credited")

        scopeA = ctx.enter_context(ExitStack())

        def sbA(name, shape, dt=F32):
            return scopeA.enter_context(nc.sbuf_tensor("a_" + name, shape, dt))

        QT = sbA("QT", [P, 2, NTOK])
        KT = sbA("KT", [P, 2, NTOK])
        V = sbA("V", [P, NPAIR, D])
        wo = sbA("wo", [P, 2, D])
        qst, kst = sbA("qst", [P, 2, 2, P]), sbA("kst", [P, 2, 2, P])
        vbd = sbA("vbd", [P, 2, H, 2, HD + 1])
        negmax = sbA("negmax", [P, 2, H])
        shift = sbA("shift", [P, 2, H, C], F32R)
        pt = sbA("pt", [P, 2, H, C])
        rsum = sbA("rsum", [P, 2, 8, 2])
        on = sbA("on", [P, 2, 2, 8, HD])
        ot = sbA("ot", [P, 2, 2, 2, C])
        scope0 = scopeA.enter_context(ExitStack())
        xT = scope0.enter_context(nc.sbuf_tensor("p_xT", [P, 2, NTOK], F32))
        wqkv = scope0.enter_context(nc.sbuf_tensor("p_wqkv", [P, 3, 2, D], F32))
        sel = scope0.enter_context(nc.sbuf_tensor("p_sel", [P, 16, P], F32))
        scope0.close()
        masked = sbA("masked", [P, 2, 2, 2, 8, P])
        qm, km = [masked[:, 1 - u, 0] for u in range(2)], [masked[:, 1 - u, 1] for u in range(2)]
        scopeA.close()
        hT = sb("hT", [P, 2, 2, NTOK], F32R)
        wgu = sb("wgu", [P, NE + 1, 2, 2, F])
        wdn = sb("wdn", [P, NE + 1, D])
        scopeX = ctx.enter_context(ExitStack())

        def sbX(name, shape, dt=F32):
            return scopeX.enter_context(nc.sbuf_tensor("x_" + name, shape, dt))

        px = sbX("px", [P, 2, 4, 2, D])
        tn = sbX("tn", [P, 2, 16, 32])
        rs = sbX("rs", [P, 2, 16])
        onx = sbX("onx", [P, 4, 2, D])
        sq = sbX("sq", [P, D])
        ms = sbX("ms", [P, 2])
        rr = sbX("rr", [P, 2])
        hx = sbX("hx", [P, 2, D])
        scopeX.close()
        scopeF = ctx.enter_context(ExitStack())

        def sbF(name, shape, dt=F32):
            return scopeF.enter_context(nc.sbuf_tensor("f_" + name, shape, dt))

        kflat = kmx[:].rearrange("p s h k -> p (s h k)")
        WE, WRING = 4 * F + D, 3
        w_r = kflat[:, 0:2 * WRING * WE].rearrange("p (s r n) -> p s r n", s=WRING, r=2)
        act_r = kflat[:, 2 * WRING * WE:2 * WRING * WE + 2048].rearrange("p (s r n) -> p s r n", s=2, r=2)
        sl = sbF("sl", [P, 2, 512])
        act = sbF("act", [P, 2, 512])
        pr = sbF("pr", [P, 2, 512])
        lT = sbF("lT", [NE, NTOK])
        lg = sbF("lg", [P, NPAIR, NE])
        lmax = sbF("lmax", [P, NPAIR])
        ex = sbF("ex", [P, NPAIR, NE])
        ahead = sbF("ahead", [P, NPAIR, NE, NE])
        rank = sbF("rank", [P, NPAIR, NE])
        wsel = sbF("wsel", [P, NPAIR, NE])
        wsum = sbF("wsum", [P, NPAIR])
        wrow = sbF("wrow", [1, 2, NTOK])
        wb = sbF("wb", [P, 2, NTOK])
        fy = sbF("fy", [P, NPAIR, D])
        fstats = sbF("fstats", [P, NPAIR, 6])
        fmv = sbF("fmv", [P, NPAIR, 2])
        fvar = sbF("fvar", [P, NPAIR])
        frstd = sbF("frstd", [P, NPAIR])
        scopeF.close()
        wT = lT

        class Chain:

            def __init__(self, eng, s):
                self.eng, self.s, self.base, self.k = eng, s, 0, 0

            def __call__(self, ins):
                self.k += 1
                ins.then_inc(self.s, 1)
                self.eng.wait_ge(self.s, self.base + self.k)

        cur = {}

        def steps(eng, chain, step, unroll, first, lo, hi, last):
            for n in range(first, unroll * lo):
                step(n, n)
            start = chain.base + chain.k if chain else 0
            with eng.Fori(lo, hi) as j:
                cur["half"] = 2 * j
                if chain:
                    chain.base, chain.k = start + (j - lo) * step.links, 0
                for k in range(unroll):
                    step(unroll * j + k, k)
                if chain:
                    assert chain.k == step.links, chain.k
            if chain:
                chain.base, chain.k = start + (hi - lo) * step.links, 0
            for n in range(unroll * hi, last + 1):
                step(n, n)

        def valid(k, m, off, count=B):
            return (not isinstance(m, int)) or 0 <= m + off < count

        def all_steps(eng, chain, a_step, x_step, x_first, f_weights, f_first, f_second):
            steps(eng, chain, a_step, 2, -1, 1, NPAIR // 2 - 1, NPAIR - 2)
            x_first()
            a_step(NPAIR - 1, NPAIR - 1)
            x_step(-4, -4)
            x_step(-3, -3)
            a_step(NPAIR, NPAIR)
            x_step(-2, -2)
            a_step(NPAIR + 1, NPAIR + 1)
            x_step(-1, -1)
            steps(eng, chain, x_step, 4, 0, 1, B // 4 - 1, B)
            f_weights()
            x_step(B + 1, B + 1)
            f_first()
            x_step(B + 2, B + 2)
            f_second()
            x_step(B + 3, B + 3)

        def pair_of(m, k, off):
            if isinstance(m, int):
                return (m + off) // 2
            return cur["half"] + (k + off) // 2

        def wait_km_staged(eng, m, k):
            if not isinstance(m, int) or m >= 0:
                for hp in range(2):
                    wait_km(eng, m, k, hp)

        def wait_mrow_free(eng, m, k, gr):
            s = ((k - 2) % 4) * 2 + gr
            if isinstance(m, int):
                if m >= 2:
                    eng.wait_ge(x_mrow[s], 16 * ((m - 2) // 4 + 1))
            else:
                eng.wait_ge(x_mrow[s], (m - k) * 4 + 16 * ((k - 2) // 4 + 1))

        def evac_phase0(eng, copy, s, first, end):
            for n in range(first, end, 2):
                eng.wait_ge(p0_mm, n + 1)
                if n < 8:
                    w, gr, hf = n // 4, (n // 2) % 2, n % 2
                    ins = copy((QT, KT)[w][:, gr, 512 * hf:512 * hf + 512], bank[:, n, :])
                else:
                    v = n - 8
                    ins = copy(V[:, 2 * v:2 * v + 2, :].rearrange("p a d -> p (a d)"), bank[:, n % 8, :])
                ins.then_inc(s, 1)

        def expert(ei):
            return NE if ei == 0 else ei - 1

        def order(i):
            return expert(i // 2), i % 2

        NI = 2 * (NE + 1)
        GU = (3, 5)
        ACC = (2, 7, 1, 0)

        def wait_km(eng, m, k, hp):
            if isinstance(m, int):
                eng.wait_ge(x_km[k % 4][hp], 32 * (m // 4 + 1))
            else:
                eng.wait_ge(x_km[k % 4][hp], (m - k) * 8 + 32 * (k // 4 + 1))

        def wait_mrow(eng, m, k, gr):
            s = (k % 4) * 2 + gr
            if isinstance(m, int):
                eng.wait_ge(x_mrow[s], 16 * (m // 4 + 1))
            else:
                eng.wait_ge(x_mrow[s], (m - k) * 4 + 16 * (k // 4 + 1))

        def s2_tile(m, k, t):
            return (m, k, t - 2) if t >= 2 else (m - 1, k - 1, t + 6)

        block = ctx.enter_context(nc.Block())

        @block.sync
        def _(sp):
            sp.dma_start(wqkv[:, 0], I["wqkv"][:, 0]).then_inc(ld_w[0], 16)
            sp.dma_start(xT[:, :, 0:512], I["xT"].rearrange("(c p) t -> p c t", p=P)[:, :, 0:512]).then_inc(ld_x[0], 16)
            sp.dma_start(xT[:, :, 512:1024], I["xT"].rearrange("(c p) t -> p c t", p=P)[:, :, 512:1024]).then_inc(ld_x[1], 16)
            sp.dma_start(wqkv[:, 1:3], I["wqkv"][:, 1:3]).then_inc(ld_w[1], 16)
            sp.dma_start(con[:, :], I["con"]).then_inc(ld_c, 16)
            sp.dma_start(sel[:].rearrange("p a b -> p (a b)"), I["sel"]).then_inc(ld_c, 16)
            sp.dma_start(wo[:], I["wo"]).then_inc(ld_xn, 16)
            sp.dma_start(x_sb[:], I["x"].rearrange("(n p) d -> p n d", p=P)).then_inc(ld_xn, 16)
            sp.dma_start(cx[:], I["ctx"].rearrange("(n p) d -> p n d", p=P)).then_inc(ld_ctx, 16)
            for o, name in ((xw, "xw"), (xwo, "xwo"), (xb, "xb")):
                sp.dma_start(o[:], I[name]).then_inc(ld_ctx, 16)
            sp.dma_start(bvb[:], I["xbv"].rearrange("(o n) -> o n", o=1).to_broadcast((P, 4 * C))).then_inc(ld_ctx, 16)
            sp.dma_start(rmsw[:], I["rms"].rearrange("(o n) -> o n", o=1).to_broadcast((P, D))).then_inc(ld_f, 16)
            sp.dma_start(rw[:], I["rw"]).then_inc(ld_f, 16)

            def x_step(m, k):
                if valid(k, m, 0):
                    sp.wait_ge(x_mte, done(2 * m + 1))
                    dst = qx[MAXROW:MAXROW + 3 * XROW + 1:XROW, k % 4, 1, :].bitcast(F32)
                    sp.dma_start(dst, mrow[:, k % 2, 1, :].bitcast(F32)).then_inc(x_mrow[(k % 4) * 2 + 1], 16)
                if valid(k, m, 2):
                    sp.wait_ge(x_stack[1], done(m + 2))
                    sp.wait_ge(x_s2, free(8 * (m + 2) + 7, 32))
                    for j in range(4):
                        r = slice(XROW * j, XROW * j + XROW)
                        sp.dma_start(kmx[r, (k + 2) % 4, j::4, :].bitcast(F32),
                                     kstage[r, k % 2, :, :].bitcast(F32)).then_inc(x_km[(k + 2) % 4][j // 2], 16)
                if valid(k, m, 1):
                    sp.wait_ge(x_mte, done(2 * (m + 1)))
                    dst = qx[MAXROW:MAXROW + 3 * XROW + 1:XROW, (k + 1) % 4, 0, :].bitcast(F32)
                    sp.dma_start(dst, mrow[:, (k + 1) % 2, 0, :].bitcast(F32)).then_inc(x_mrow[((k + 1) % 4) * 2], 16)
                if isinstance(m, int) and m == 3:
                    sp.wait_ge(a_x1, done(NPAIR - 1))
                    load_expert(NE)
                if valid(k, m, -4, NE):
                    load_expert(m - 4)

            def load_expert(e):
                for o, name in ((wgu, "wgu"), (wdn, "wdn")):
                    sp.dma_start(o[:, bass.ds(e, 1)], I[name][:, bass.ds(e, 1)]).then_inc(ld_f2, 16)

            for n in (-3, -2, -1):
                x_step(n, n)
            steps(sp, None, x_step, 4, 0, 1, B // 4 - 1, B)

            sp.wait_ge(f_wT, done(0))
            for e in range(NE):
                sp.wait_ge(f_wb, free(e, 2))
                sp.dma_start(wrow[:, e % 2, :], wT[e:e + 1, :]).then_inc(f_wrow[e % 2], 16)
            for t in range(0, NPAIR, 2):
                sp.wait_ge(f_o, done(t + 1))
                sp.dma_start(out.rearrange("(n p) d -> p n d", p=P)[:, t:t + 2, :], fy[:, t:t + 2, :]).then_inc(st_out, 16)
            sp.wait_ge(st_out, 8 * NPAIR)

        @block.gpsimd
        def _(pool):
            g = nc.gpsimd
            link = Chain(pool, pool_link)
            for s in credit.values():
                pool.sem_inc(s, CREDIT)
            pool.sem_inc(credited, 1)
            g.memset(half[:, 0:1], -0.5)
            g.memset(half[:, 1:2], LN_EPS)
            g.memset(half[:, 2:3], RMS_EPS)
            g.memset(half[:, 3:4], 1.0 / D)
            g.memset(kmx[:].bitcast(F32), 0.0).then_inc(zeroed, 1)
            link(g.memset(vst[:], 0.0))
            g.memset(vst[:, :, :, :, :, XD:XD + 1], 1.0).then_inc(zeroed, 1)
            pool.wait_ge(ld_c, 32)
            pool.wait_ge(consts_ready, 1)
            pool.wait_ge(p0_act, 4)
            pool.wait_ge(p0_dve, 4)

            def rstd_of(v, eps_col, o, w):
                link(g.tensor_tensor(o, v, half[:, eps_col:eps_col + 1].to_broadcast((P, w)), ALU.add))
                return g.tensor_tensor(o, o, half[:, 0:1].to_broadcast((P, w)), ALU.pow)

            def a_step(n, k):
                if valid(k, n, 1, NPAIR):
                    u = (k + 1) % 2
                    pool.wait_ge(a_s2, free(n + 1, 2))
                    for gr in range(2):
                        g.tensor_tensor(qm[u][:, gr],
                                        QT[:, gr, bass.ds((n + 1) * P, P)].rearrange("p (o t) -> p o t", o=1).to_broadcast((P, 8, P)),
                                        K("headmask").rearrange("p (h o) -> p h o", o=1).to_broadcast((P, 8, P)),
                                        ALU.mult).then_inc(a_qm, 1)
                if valid(k, n, -2, NPAIR):
                    u = k % 2
                    pool.wait_ge(a_var, done(n - 2))
                    rstd_of(mv[:, u, 1:2], 1, rstd[:, u:u + 1], 1).then_inc(a_rstd, 1)
                if valid(k, n, 2, NPAIR):
                    u = k % 2
                    pool.wait_ge(a_s1, free(n + 2, 2))
                    if isinstance(n, int) and n == -1:
                        pool.wait_ge(p0_mm, 12)
                    g.tensor_tensor(km[u][:, 1],
                                    KT[:, 1, bass.ds((n + 2) * P, P)].rearrange("p (o t) -> p o t", o=1).to_broadcast((P, 8, P)),
                                    K("headmask").rearrange("p (h o) -> p h o", o=1).to_broadcast((P, 8, P)),
                                    ALU.mult).then_inc(a_km[1], 1)
            a_step.links = 2
            def x_step(m, k):
                if k % 2 and valid(k, m, 3):
                    n = pair_of(m, k, 3)
                    for w in range(2):
                        pool.wait_ge(x_ropes, done(2 * n + w))
                        pool.wait_ge(x_lo, free(2 * n + w, 2))
                        g.tensor_tensor(roped[:, w], rope[:, w, 0], rope[:, w, 1], ALU.add).then_inc(x_roped, 1)
                    for w in range(2):
                        pool.wait_ge(x_hi, done(2 * n + w))
                        g.tensor_tensor(hilo[:, ((k + 3) // 2) % 2, w, 1], roped[:, w], hilo[:, ((k + 3) // 2) % 2, w, 0].bitcast(F32),
                                        ALU.subtract).then_inc(x_lo, 1)
                if k % 2 == 0 and valid(k, m, -4):
                    n = pair_of(m, k, -4)
                    pool.wait_ge(x_var, done(n))
                    rstd_of(mv[:, 0, 1:2], 1, rstd[:, 0:1], 1).then_inc(x_rstd, 1)
                if k % 2 == 0 and valid(k, m, -4):
                    n, u = pair_of(m, k, -4), ((k - 4) // 2) % 2
                    pool.wait_ge(x_sq, done(n))
                    link(g.tensor_tensor(ms[:, u:u + 1], ms[:, u:u + 1], half[:, 3:4], ALU.mult))
                    rstd_of(ms[:, u:u + 1], 2, rr[:, u:u + 1], 1).then_inc(x_rr, 1)
            x_step.links = 2 + 4

            def split_weights(ei):
                pool.wait_ge(f_whi, done(ei))
                e = expert(ei)
                g.tensor_tensor(w_r[:, ei % WRING, 1, 0:4 * F], wgu[:, e].rearrange("p u c f -> p (u c f)"),
                                w_r[:, ei % WRING, 0, 0:4 * F].bitcast(F32), ALU.subtract)
                g.tensor_tensor(w_r[:, ei % WRING, 1, 4 * F:WE], wdn[:, e], w_r[:, ei % WRING, 0, 4 * F:WE].bitcast(F32),
                                ALU.subtract).then_inc(f_wlo, 1)

            a_step(-2, -2)
            def f_weights():
                split_weights(0)
                split_weights(1)

            nothing = lambda: None
            all_steps(pool, link, a_step, x_step, nothing, f_weights, nothing, nothing)

            for ei in range(1, NE + 1):
                e = expert(ei)
                if ei < NE:
                    split_weights(ei + 1)
                pool.wait_ge(f_wrow[e % 2], 16 * (e // 2 + 1))
                pool.wait_ge(f_act, free(2 * e + 3, 4))
                g.partition_broadcast(wb[:, e % 2, :], wrow[0:1, e % 2, :]).then_inc(f_wb, 1)
            for b in range(NPAIR // 2):
                pool.wait_ge(f_var, done(b))
                t = slice(2 * b, 2 * b + 2)
                rstd_of(fmv[:, t, 1], 1, frstd[:, t], 2).then_inc(f_rstd, 1)

        @block.scalar
        def _(sc):
            a = nc.scalar

            def a_step(n, k):
                if valid(k, n, 0, NPAIR):
                    u = k % 2
                    sc.wait_ge(a_pv, free(n, 2))
                    for b in range(2):
                        t = slice(64 * b, 64 * b + 64)
                        last = a.copy(vbd[t, u, :, b, 0:HD], V[t, bass.ds(n, 1), :].rearrange("p o (h d) -> p (o h) d", h=H))
                    last.then_inc(a_vbd, 1)
                    for gr in range(2):
                        sc.wait_ge((a_s2_first, a_s2)[gr], done(n))
                        a.activation(pt[:, u, 8 * gr:8 * gr + 8].rearrange("p h q -> p (h q)"), bank[:, 2 + gr, :],
                                     ACT.Exp, scale=float(HD) ** -0.5).then_inc((a_pt_first, a_pt)[gr], 1)
                if valid(k, n, 2, NPAIR):
                    u, tok = k % 2, bass.ds((n + 2) * P, P)
                    sc.wait_ge(a_s2, free(n + 2, 2))
                    a.copy(qst[:, u], QT[:, :, tok]).then_inc(a_st, 1)
                    a.copy(kst[:, u], KT[:, :, tok]).then_inc(a_st, 1)
                if valid(k, n, -1, NPAIR):
                    u = (k - 1) % 2
                    sc.wait_ge(a_t, done(n - 1))
                    sc.wait_ge(a_y, free(n - 1, 2))
                    a.copy(ot[:, u].rearrange("p h b q -> p b h q"),
                           bank[:, 5, 0:256].rearrange("p (b h q) -> p b h q", b=2, h=2)).then_inc(a_ot, 1)
            evac_phase0(sc, lambda o, i: a.copy(o, i), p0_act, 0, 8)
            sc.wait_ge(p0_dve, 4)
            sc.wait_ge(p0_act, 4)
            sc.wait_ge(vbd_zero, 1)
            sc.wait_ge(credited, 1)
            a_step(-2, -2)
            evac_phase0(sc, lambda o, i: a.copy(o, i), p0_act, 8, 12)
            sc.wait_ge(p0_dve, 6)
            sc.wait_ge(p0_act, 6)

            def evac_m(m, k, gr):
                sc.wait_ge(x_mt, done(2 * m + gr))
                wait_mrow_free(sc, m, k, gr)
                a.copy(mrow[:, k % 2, gr, :], bank[0:4, 2, 0:256]).then_inc(x_mte, 1)

            def x_step(m, k):
                for t in range(8):
                    mb, kb, tb = s2_tile(m, k, t)
                    if valid(kb, mb, 0):
                        i = 8 * mb + tb
                        sc.wait_ge(x_s2, done(i))
                        if tb % 4 == 0:
                            sc.wait_ge(x_pv, free(2 * mb + tb // 4, 2))
                        a.activation(px[:, tb // 4, tb % 4].rearrange("p c q -> p (c q)"), bank[:, 5 + t % 2, :], ACT.Exp,
                                     scale=float(XD) ** -0.5).then_inc(x_exp, 1)
                    if t == 1 and valid(k, m, 0):
                        evac_m(m, k, 1)
                    if t == 2 and valid(k, m, 2):
                        sc.wait_ge(x_spread[1], done(m + 2))
                        wait_km_staged(sc, m, k)
                        a.activation(kstage[:, k % 2], bank[:, 1, :].rearrange("p (g q) -> p g q", g=2),
                                     ACT.Identity, bias=K("onescol")).then_inc(x_stack[1], 1)
                    if t == 3 and valid(k, m, 2):
                        sc.wait_ge(x_spread[0], done(m + 2))
                        sc.wait_ge(x_s2, free(8 * (m + 2) + 7, 32))
                        a.copy(qx[:, (k + 2) % 4], bank[:, 0, :].rearrange("p (g q) -> p g q", g=2)).then_inc(x_stack[0], 1)
                    if t == 0 and k % 2 and valid(k, m, 1):
                        n = pair_of(m, k, 1)
                        sc.wait_ge(x_v, free(n, 1))
                        a.copy(cst[:], cx[:, bass.ds(n, 1), :].rearrange("p o d -> p (o d)")).then_inc(x_cst, 1)
                    if t == 7 and k % 2 and valid(k, m, 3):
                        n = pair_of(m, k, 3)
                        for w in range(2):
                            sc.wait_ge(x_roped, done(2 * n + w))
                            sc.wait_ge(x_spread[w], free(2 * n + 1, 4))
                            a.copy(hilo[:, ((k + 3) // 2) % 2, w, 0], roped[:, w]).then_inc(x_hi, 1)
                    if t == 5 and valid(k, m, 1):
                        evac_m(m + 1, k + 1, 0)
                    if t == 5 and k % 2 == 0 and valid(k, m, -4):
                        n, u = pair_of(m, k, -4), ((k - 4) // 2) % 2
                        sc.wait_ge(x_x2, done(n))
                        if not (isinstance(n, int) and n == 0):
                            sc.wait_ge(x_sq, free(n, 1))
                        sc.wait_ge(x_rr, free(n, 2))
                        a.activation(sq[:], x_sb[:, bass.ds(n, 1), :].rearrange("p o d -> p (o d)"), ACT.Square,
                                     accum_out=ms[:, u:u + 1]).then_inc(x_sq, 1)
                    if t == 6 and k % 2 and valid(k, m, -5):
                        n = pair_of(m, k, -5)
                        sc.wait_ge(x_ht, done(n))
                        a.copy(hT[:, 0, :, bass.ds(n * P, P)], bank[:, 0, 0:D].rearrange("p (c t) -> p c t", c=2)).then_inc(x_hhi, 1)

            def split_weights(ei):
                e = expert(ei)
                sc.wait_ge(f_dn, free(2 * ei + 1, 2 * WRING))
                a.copy(w_r[:, ei % WRING, 0, 0:4 * F], wgu[:, e].rearrange("p u c f -> p (u c f)"))
                a.copy(w_r[:, ei % WRING, 0, 4 * F:WE], wdn[:, e]).then_inc(f_whi, 1)

            def x_first():
                sc.wait_ge(ld_ctx, 16 * 5)

            def f_weights():
                sc.wait_ge(x_s2, done(8 * B - 1))
                sc.wait_ge(ld_f2, 32 * (NE + 1))
                split_weights(0)
                split_weights(1)

            def silu_of(i):
                sc.wait_ge(f_gu[i % 2], done(i // 2))
                sc.wait_ge(f_prod, free(i, 2))
                a.activation(sl[:, i % 2], bank[:, GU[i % 2], :], ACT.Silu).then_inc(f_silu, 1)

            def high_part_of(i):
                sc.wait_ge(f_act, done(i))
                sc.wait_ge(f_dn, free(i, 2))
                a.copy(act_r[:, i % 2, 0], act[:, i % 2]).then_inc(f_ahi, 1)

            def logits_rows(hf):
                sc.wait_ge(f_lt, done(hf))
                a.copy(lT[:, 512 * hf:512 * hf + 512], bank[0:NE, 5 + hf, :]).then_inc(f_lte, 1)

            def f_second():
                silu_of(0)

            all_steps(sc, None, a_step, x_step, x_first, f_weights, lambda: None, f_second)

            high_part_of(0)
            logits_rows(0)
            logits_rows(1)
            split_weights(2)
            sc.wait_ge(f_lsub, done(0))
            a.activation(ex[:], lg[:], ACT.Exp).then_inc(f_exp, 1)
            silu_of(1)
            high_part_of(1)
            sc.wait_ge(f_wtp, done(0))
            for hf in range(2):
                last = a.copy(wT[:, 512 * hf:512 * hf + 512], bank[32 * hf:32 * hf + NE, 0, :])
            last.then_inc(f_wT, 1)
            for i in range(2, NI):
                silu_of(i)
                high_part_of(i)
                if i % 2 == 0 and i // 2 + 2 <= NE:
                    split_weights(i // 2 + 2)

        @block.vector
        def _(ve):
            v = nc.vector
            link = Chain(ve, dve_link)
            link(v.memset(vbd[:], 0.0))
            v.memset(vbd[0:64, :, :, 0, HD:HD + 1], 1.0)
            v.memset(vbd[64:128, :, :, 1, HD:HD + 1], 1.0).then_inc(vbd_zero, 1)
            ve.wait_ge(ld_c, 32)
            v.tensor_copy(sel_r[:], sel[:])
            v.tensor_copy(sameb_r[:], K("sameb")).then_inc(consts_ready, 1)
            def statistics(src, u, sem_var, bn_n):
                v.bn_stats(stats[:, u], src).then_inc(bn_done, 1)
                ve.wait_ge(bn_done, done(bn_n))
                v.memset(wait_here[:], 0.0)
                v.bn_aggr(mv[:, u], stats[:, u]).then_inc(sem_var, 1)

            def normalised(o, src, u, sem_rstd, n):
                ve.wait_ge(sem_rstd, done(n))
                return v.tensor_scalar(o, src, mv[:, u, 0:1], rstd[:, u:u + 1], ALU.subtract, ALU.mult)

            def a_step(n, k):
                if valid(k, n, -1, NPAIR):
                    u = (k - 1) % 2
                    ve.wait_ge(a_pv, done(n - 1))
                    o = bank[:, 4, 0:8 * 2 * (HD + 1)].rearrange("p (h b d) -> p h b d", h=8, b=2)
                    link(v.reciprocal(rsum[:, u], o[:, :, :, HD]))
                    ve.wait_ge(a_t, free(n - 1, 2))
                    for b in range(2):
                        last = v.tensor_tensor(on[:, u, b], o[:, :, b, 0:HD],
                                               rsum[:, u, :, b:b + 1].to_broadcast((P, 8, HD)), ALU.mult)
                    last.then_inc(a_on, 1)
                if valid(k, n, 2, NPAIR):
                    u = k % 2
                    ve.wait_ge(a_s1, free(n + 2, 2))
                    v.tensor_tensor(km[u][:, 0],
                                    KT[:, 0, bass.ds((n + 2) * P, P)].rearrange("p (o t) -> p o t", o=1).to_broadcast((P, 8, P)),
                                    K("headmask").rearrange("p (h o) -> p h o", o=1).to_broadcast((P, 8, P)),
                                    ALU.mult).then_inc(a_km[0], 1)
                if valid(k, n, -2, NPAIR):
                    u = k % 2
                    ve.wait_ge(a_y, done(n - 2))
                    v.tensor_tensor(ysum[:, u], bank[:, 6 + u, 0:D], x_sb[:, bass.ds(n - 2, 1), :].rearrange("p o d -> p (o d)"),
                                    ALU.add).then_inc(a_sum, 1)
                    ve.wait_ge(a_sum, done(n - 2))
                    statistics(ysum[:, u], u, a_var, n - 2)
                if valid(k, n, 1, NPAIR):
                    u = (k + 1) % 2
                    ve.wait_ge(a_s1, done(n + 1))
                    v.tensor_reduce(negmax[:, u], bank[:, 0:2, :].rearrange("p a (h k) -> p (a h) k", k=C), AX.X, ALU.max,
                                    negate=True).then_inc(a_max, 1)
                    ve.wait_ge(a_max, done(n + 1))
                    ve.wait_ge(a_s2, free(n + 1, 2))
                    v.tensor_tensor(shift[:, u], K("fold").rearrange("p (o q) -> p o q", o=1).to_broadcast((P, H, C)),
                                    negmax[:, u].rearrange("p (h o) -> p h o", o=1).to_broadcast((P, H, C)),
                                    ALU.mult).then_inc(a_shift, 1)
                if valid(k, n, -2, NPAIR):
                    u = k % 2
                    normalised(x_sb[:, bass.ds(n - 2, 1), :].rearrange("p o d -> p (o d)"), ysum[:, u], u, a_rstd,
                               n - 2).then_inc(a_x1, 1)
            a_step.links = 2
            evac_phase0(ve, lambda o, i: v.tensor_copy(o, i), p0_dve, 1, 8)
            ve.wait_ge(p0_act, 4)
            ve.wait_ge(p0_dve, 4)
            ve.wait_ge(credited, 1)
            a_step(-2, -2)
            ve.wait_ge(zeroed, 2)
            ve.wait_ge(ld_ctx, 16 * 5)
            ve.wait_ge(ld_f, 32)
            link(v.tensor_copy(rw_r[:, 0], rw[:]))
            v.tensor_tensor(rw_r[:, 1], rw[:], rw_r[:, 0].bitcast(F32), ALU.subtract).then_inc(rw_ready, 1)
            for n in (1, 3):
                link(v.tensor_tensor(xw[:, n], xw[:, n], K("signrow"), ALU.mult))
                link(v.tensor_tensor(xb[:, n:n + 1], xb[:, n:n + 1], K("signcol"), ALU.mult))
            ve.sem_inc(x_consts, 1)
            evac_phase0(ve, lambda o, i: v.tensor_copy(o, i), p0_dve, 9, 12)
            ve.wait_ge(ld_xn, 32)

            def x_step(m, k):
                for t in range(8):
                    if valid(k, m, 1):
                        ve.wait_ge(x_s1, done(8 * (m + 1) + t))
                        if t % 4 == 0:
                            ve.wait_ge(x_mt, free(2 * (m + 1) + t // 4, 4))
                        v.tensor_reduce(nmax[:, (k + 1) % 2, t // 4, (t // 2) % 2, 2 * (t % 2):2 * (t % 2) + 2],
                                        bank[:, 3 + t % 2, :].rearrange("p (h k) -> p h k", h=2), AX.X, ALU.max,
                                        negate=True).then_inc(x_max, 1)
                    s = (k - 1) % 2
                    if t == 5 and valid(k, m, -1):
                        ve.wait_ge(x_pv, done(2 * (m - 1) + 1))
                        v.transpose(tn[:, s].rearrange("p a b -> p (a b)"), bank[:, 7, :]).then_inc(x_n1, 1)
                    if t == 6 and valid(k, m, -1):
                        ve.wait_ge(x_n1, done(m - 1))
                        link(v.reciprocal(rs[:, s], tn[:, s, :, XD]))
                        v.tensor_tensor(tn[:, s, :, 0:XD], tn[:, s, :, 0:XD],
                                        rs[:, s].rearrange("p (a o) -> p a o", o=1).to_broadcast((P, 16, XD)), ALU.mult).then_inc(x_n2, 1)
                    if t == 7 and valid(k, m, -1):
                        ve.wait_ge(x_n2, done(m - 1))
                        v.transpose(onx[:, (k - 1) % 4].rearrange("p g q -> p (g q)"),
                                    tn[:, s].rearrange("p a b -> p (a b)")).then_inc(x_norm, 1)
                    if (t == 7 and k % 2 == 0 and valid(k, m, 4)) or (t == 0 and k % 2 and valid(k, m, 3)):
                        n = pair_of(m, k, 4 if t == 7 else 3)
                        for w in (0 if t == 7 else 1,):
                            ve.wait_ge((x_pq, x_pk)[w], done(2 * n + 1))
                            ve.wait_ge(x_roped, free(2 * n + w, 2))
                            for r in range(2):
                                last = v.scalar_tensor_tensor(rope[:, w, r], bank[:, w, 256 * r:256 * r + 256],
                                                              xb[:, 2 * w + r:2 * w + r + 1], K(("cos", "sin")[r]), ALU.add, ALU.mult)
                            last.then_inc(x_ropes, 1)
                    if t == 7 and k % 2 and valid(k, m, 1):
                        n = pair_of(m, k, 1)
                        ve.wait_ge(x_v, done(n))
                        ve.wait_ge(x_pv, free(4 * n + 3, 8))
                        v.tensor_tensor(vst[:, ((k + 1) // 2) % 2].rearrange("p c b h r -> p (c b h) r")[:, :, 0:XD],
                                        bank[:, 2, 0:D].rearrange("p (n d) -> p n d", d=XD),
                                        bvb[:].rearrange("p (n d) -> p n d", d=XD), ALU.add).then_inc(x_vst, 1)
                    if t == 0 and k % 2 == 0 and valid(k, m, -4):
                        n = pair_of(m, k, -4)
                        ve.wait_ge(x_y, done(n))
                        xs = x_sb[:, bass.ds(n, 1), :].rearrange("p o d -> p (o d)")
                        v.scalar_tensor_tensor(ysum[:, 0], bank[:, 1, 0:D], xb[:, 4:5], xs, ALU.add, ALU.add).then_inc(x_ysum, 1)
                        ve.wait_ge(x_ysum, done(n))
                        statistics(ysum[:, 0], 0, x_var, NPAIR + n)
                    if t == 7 and k % 2 and valid(k, m, -5):
                        n = pair_of(m, k, -5)
                        ve.wait_ge(x_hhi, done(n))
                        tok = bass.ds(n * P, P)
                        v.tensor_tensor(hT[:, 1, :, tok], bank[:, 0, 0:D].rearrange("p (c t) -> p c t", c=2),
                                        hT[:, 0, :, tok].bitcast(F32), ALU.subtract).then_inc(x_hlo, 1)
                    if t == 2 and k % 2 and valid(k, m, -5):
                        n, u = pair_of(m, k, -5), ((k - 5) // 2) % 2
                        ve.wait_ge(x_rr, done(n))
                        ve.wait_ge(x_ht, free(n, 2))
                        v.scalar_tensor_tensor(hx[:, u], x_sb[:, bass.ds(n, 1), :].rearrange("p o d -> p (o d)"), rr[:, u:u + 1],
                                               rmsw[:], ALU.mult, ALU.mult).then_inc(x_h, 1)
                    if t == 3 and k % 2 == 0 and valid(k, m, -4):
                        n = pair_of(m, k, -4)
                        normalised(x_sb[:, bass.ds(n, 1), :].rearrange("p o d -> p (o d)"), ysum[:, 0], 0, x_rstd, n).then_inc(x_x2, 1)
            x_step.links = 4

            nothing = lambda: None
            all_steps(ve, link, a_step, x_step, nothing, nothing, nothing, nothing)

            def item(i):
                e, hf = order(i)
                ve.wait_ge(f_silu, done(i))
                ve.wait_ge(f_alo, free(i, 2))
                dst = act[:, i % 2] if e == NE else pr[:, i % 2]
                prod = v.tensor_tensor(dst, bank[:, GU[i % 2] + 1, :], sl[:, i % 2], ALU.mult)
                prod.then_inc(f_prod, 1)
                ve.wait_ge(f_prod, done(i))
                if e == NE:
                    ve.sem_inc(f_act, 1)
                else:
                    ve.wait_ge(f_wb, done(e))
                    v.tensor_tensor(act[:, i % 2], pr[:, i % 2], wb[:, e % 2, 512 * hf:512 * hf + 512], ALU.mult).then_inc(f_act, 1)
                ve.wait_ge(f_ahi, done(i))
                v.tensor_tensor(act_r[:, i % 2, 1], act[:, i % 2], act_r[:, i % 2, 0].bitcast(F32), ALU.subtract).then_inc(f_alo, 1)

            item(0)
            ve.wait_ge(f_lg, done(0))
            lps = bank[:, 0, 0:NPAIR * NE].rearrange("p (t e) -> p t e", e=NE)
            link(v.tensor_reduce(lmax[:], lps, AX.X, ALU.max))
            v.tensor_tensor(lg[:], lps, lmax[:].rearrange("p (t o) -> p t o", o=1).to_broadcast((P, NPAIR, NE)),
                            ALU.subtract).then_inc(f_lsub, 1)
            ve.wait_ge(f_lsub, done(0))
            for e in range(NE):
                if e > 0:
                    v.tensor_tensor(ahead[:, :, e, 0:e], lg[:, :, 0:e], lg[:, :, e:e + 1].to_broadcast((P, NPAIR, e)), ALU.is_ge)
                last = v.tensor_tensor(ahead[:, :, e, e:NE], lg[:, :, e:NE], lg[:, :, e:e + 1].to_broadcast((P, NPAIR, NE - e)),
                                       ALU.is_gt)
            link(last)
            link(v.tensor_reduce(rank[:], ahead[:], AX.X, ALU.add))
            ve.wait_ge(f_exp, done(0))
            link(v.scalar_tensor_tensor(wsel[:], rank[:], 2.0, ex[:], ALU.is_lt, ALU.mult))
            link(v.tensor_reduce(wsum[:], wsel[:], AX.X, ALU.add))
            link(v.reciprocal(lmax[:], wsum[:]))
            v.tensor_tensor(wsel[:], wsel[:], lmax[:].rearrange("p (t o) -> p t o", o=1).to_broadcast((P, NPAIR, NE)),
                            ALU.mult).then_inc(f_w, 1)
            for i in range(1, NI):
                item(i)
            def normalise(b):
                ve.wait_ge(f_rstd, done(b))
                for t in (2 * b, 2 * b + 1):
                    v.tensor_scalar(fy[:, t], bank[:, ACC[b], D * (t % 2):D * (t % 2) + D], fmv[:, t, 0:1], frstd[:, t:t + 1],
                                    ALU.subtract, ALU.mult).then_inc(f_o, 1)

            for b in range(NPAIR // 2):
                ve.wait_ge(f_sum, done(b))
                tiles = (2 * b, 2 * b + 1)
                acc = {t: bank[:, ACC[t // 2], D * (t % 2):D * (t % 2) + D] for t in tiles}
                for t in tiles:
                    last = v.bn_stats(fstats[:, t], acc[t])
                link(last)
                for t in tiles:
                    last = v.bn_aggr(fmv[:, t], fstats[:, t])
                last.then_inc(f_var, 1)
                if b > 0:
                    normalise(b - 1)
            normalise(NPAIR // 2 - 1)

        @block.tensor
        def _(pe):
            mm = nc.tensor.matmul
            for n in range(12):
                pe.wait_ge(ld_w[n >= 4], 16)
                pe.wait_ge(ld_x[n % 2], 16)
                if n >= 8:
                    pe.wait_ge((p0_act, p0_dve)[n % 2], (n - 8) // 2 + 1)
                for part in range(1 if n < 8 else 2):
                    for c in range(2):
                        if n < 8:
                            w, gr, hf = n // 4, (n // 2) % 2, n % 2
                            last = mm(bank[:, n, :], wqkv[:, w, c, P * gr:P * gr + P], xT[:, c, 512 * hf:512 * hf + 512],
                                      start=c == 0, stop=c == 1)
                        else:
                            t = 2 * (n - 8) + part
                            last = mm(bank[:, n % 8, D * part:D * part + D], xT[:, c, P * t:P * t + P], wqkv[:, 2, c, :],
                                      start=c == 0, stop=c == 1)
                last.then_inc(p0_mm, 1)
            pe.wait_ge(consts_ready, 1)
            pe.wait_ge(credited, 1)
            pe.wait_ge(ld_xn, 32)

            def a_step(n, k):
                u = k % 2
                if valid(k, n, -1, NPAIR):
                    w = (k - 1) % 2
                    pe.wait_ge(a_vbd, done(n - 1))
                    pe.wait_ge(a_on, free(n - 1, 1))
                    for h in range(H):
                        if h % 8 == 0:
                            pe.wait_ge((a_pt_first, a_pt)[h // 8], done(n - 1))
                        o = 34 * (h // 2)
                        last = mm(bank[64 * (h % 2):64 * (h % 2) + 64, 4, o:o + 34], pt[:, w, h, :],
                                  vbd[:, w, h].rearrange("p b d -> p (b d)"), start=True, stop=True, skip_group_check=True)
                    last.then_inc(a_pv, 1)
                if isinstance(n, int) and n <= 0:
                    pe.wait_ge(p0_act, 6 + min(n, 0))
                    pe.wait_ge(p0_dve, 6 + min(n, 0))
                if valid(k, n, 1, NPAIR):
                    w = (k + 1) % 2
                    pe.wait_ge(a_st, done(2 * n + 3))
                    pe.wait_ge(a_max, free(n + 1, 1))
                    for gr in range(2):
                        pe.wait_ge(a_km[gr], done(n + 1))
                        for b in range(2):
                            t = slice(64 * b, 64 * b + 64)
                            last = mm(bank[t, gr, :], qst[:, w, gr, t], km[w][:, gr, :, t], start=True, stop=True)
                    last.then_inc(a_s1, 1)
                if valid(k, n, -2, NPAIR):
                    pe.wait_ge(a_ot, done(n - 2))
                    pe.wait_ge(a_sum, free(n - 2, 2))
                    for h2 in range(2):
                        last = mm(bank[:, 6 + u, 0:D], ot[:, u, h2].rearrange("p b q -> p (b q)"), wo[:, h2, :], start=h2 == 0, stop=h2 == 1)
                    last.then_inc(a_y, 1)
                if valid(k, n, 0, NPAIR):
                    pe.wait_ge(a_shift, done(n))
                    pe.wait_ge(a_qm, done(2 * n + 1))
                    pe.wait_ge(a_pt, free(n, 1))
                    for gr in range(2):
                        mm(bank[:, 2 + gr, :], sameb_r[:], shift[:, u, 8 * gr:8 * gr + 8, :], start=True, stop=False, skip_group_check=True)
                        for b in range(2):
                            t = slice(64 * b, 64 * b + 64)
                            last = mm(bank[t, 2 + gr, :], kst[:, u, gr, t], qm[u][:, gr, :, t], start=False, stop=True,
                                      skip_group_check=True)
                        last.then_inc((a_s2_first, a_s2)[gr], 1)
                if valid(k, n, -1, NPAIR):
                    w = (k - 1) % 2
                    pe.wait_ge(a_on, done(n - 1))
                    pe.wait_ge(a_ot, free(n - 1, 1))
                    for b in range(2):
                        last = nc.tensor.transpose(bank[:, 5, P * b:P * b + P], on[:, w, b].rearrange("p h d -> p (h d)"), K("ident"))
                    last.then_inc(a_t, 1)

            def maxima_rows(m, k, gr):
                pe.wait_ge(x_max, done(8 * m + 4 * gr + 3))
                if gr == 1 and k % 2 == 0:
                    pe.wait_ge(x_vst, done(pair_of(m, k, 0)))
                else:
                    pe.wait_ge(x_mte, free(2 * m + gr, 1))
                for c in range(2):
                    last = nc.tensor.transpose(bank[0:4, 2, P * c:P * c + P], nmax[:, k % 2, gr, c, :], K("ident"))
                last.then_inc(x_mt, 1)

            def weighted_values(m, k, gr, c):
                if c == 0:
                    pe.wait_ge(x_exp, done(8 * m + 4 * gr + 3))
                if gr == 0 and c == 0:
                    pe.wait_ge(x_vst, done(pair_of(m, k, 0)))
                    pe.wait_ge(x_n1, free(m, 1))
                for j in range(4):
                    last = mm(bank[XROW * j:XROW * j + XROW, 7, D * gr:D * gr + D], vst[:, (k // 2) % 2, c, k % 2, 4 * gr + j, :],
                              px[:, gr, j, c, :], start=c == 0, stop=c == 1, skip_group_check=True)
                if c == 1:
                    last.then_inc(x_pv, 1)

            def project(m, k, w, r):
                n = pair_of(m, k, 4)
                if w == 0 and r == 0 and isinstance(m, int) and m < 0:
                    pe.wait_ge(a_x1, done(n))
                if r == 0:
                    pe.wait_ge(x_stack[w], free(2 * n, 2))
                src = (x_sb, cx)[w][:, bass.ds(n, 1), :].rearrange("p o d -> p (o d)")
                mm(bank[:, w, D * r:D * r + D], xw[:, 2 * w + r, :], src, start=True, stop=True,
                   skip_group_check=True).then_inc((x_pq, x_pk)[w], 1)

            def x_step(m, k):
                if isinstance(m, int) and m == -1:
                    pe.wait_ge(a_pt, done(NPAIR - 1))
                    pe.wait_ge(a_on, done(NPAIR - 1))
                for t in range(8):
                    if valid(k, m, 1):
                        m1, s = m + 1, (k + 1) % 4
                        gr, c, hp = t // 4, (t // 2) % 2, t % 2
                        if t == 0:
                            pe.wait_ge(x_stack[0], done(m1))
                        if t < 2:
                            wait_km(pe, m1, k + 1, t)
                        pe.wait_ge(x_max, free(8 * m1 + t, 2))
                        mm(bank[:, 3 + t % 2, :], qx[:, s, gr, P * c:P * c + P],
                           kmx[:, s, 4 * gr + 2 * hp:4 * gr + 2 * hp + 2, :].rearrange("p h k -> p (h k)"),
                           start=True, stop=True).then_inc(x_s1, 1)
                    mb, kb, tb = s2_tile(m, k, t)
                    if valid(kb, mb, 0):
                        s, gr = kb % 4, tb // 4
                        if tb % 4 == 0:
                            wait_mrow(pe, mb, kb, gr)
                        pe.wait_ge(x_exp, free(8 * mb + tb, 2))
                        for c in range(2):
                            last = mm(bank[:, 5 + t % 2, D * c:D * c + D], kmx[:, s, tb, P * c:P * c + P], qx[:, s, gr, :],
                                      start=True, stop=True, skip_group_check=True)
                        last.then_inc(x_s2, 1)
                    if t == 7 and k % 2 and valid(k, m, -3):
                        n = pair_of(m, k, -3)
                        pe.wait_ge(x_norm, done(2 * n + 1))
                        if valid(k, m, 2):
                            pe.wait_ge(x_stack[1], done(m + 2))
                        for gr in range(2):
                            for b in range(2):
                                last = mm(bank[64 * b:64 * b + 64, 1, 0:D], xwo[:, gr, :], onx[:, (k - 3 + b) % 4, gr, :],
                                          start=gr == 0, stop=gr == 1, skip_group_check=True)
                        last.then_inc(x_y, 1)
                    if t == 0 and valid(k, m, -1):
                        weighted_values(m - 1, k - 1, 0, 1)
                    if t == 1 and valid(k, m, 0):
                        maxima_rows(m, k, 1)
                    if t == 2 and valid(k, m, 2):
                        n = pair_of(m, k, 2)
                        b = k % 2
                        slot = ((k + 2) // 2) % 2
                        for w in (1, 0):
                            pe.wait_ge(x_lo, done(2 * n + w))
                            if k % 2 and valid(k, m, 3):
                                pe.wait_ge(x_ropes, done(2 * pair_of(m, k, 3) + w))
                            elif k % 2:
                                pe.wait_ge(x_stack[w], free(m + 2, 1))
                            elif w == 0 and valid(k, m, -6):
                                pe.wait_ge(x_hlo, done(pair_of(m, k, -6)))
                            elif w == 1 and valid(k, m, -4):
                                pe.wait_ge(x_ysum, done(pair_of(m, k, -4)))
                            else:
                                pe.wait_ge(x_stack[w], free(m + 2, 1))
                                pe.wait_ge(x_ropes, done(2 * pair_of(m, k, 2) + w))
                            for gr in range(2):
                                for part in range(2):
                                    last = mm(bank[:, w, D * gr:D * gr + D], sel_r[:, ((w * 2 + b) * 2 + gr) * 2 + part, :],
                                              hilo[:, slot, w, part, :], start=part == 0, stop=part == 1, skip_group_check=True)
                            last.then_inc(x_spread[w], 1)
                    if t == 5 and k % 2 and valid(k, m, -5):
                        n, u = pair_of(m, k, -5), ((k - 5) // 2) % 2
                        pe.wait_ge(x_h, done(n))
                        if valid(k, m, 2):
                            pe.wait_ge(x_stack[0], done(m + 2))
                        for c in range(2):
                            last = nc.tensor.transpose(bank[:, 0, P * c:P * c + P], hx[:, u, P * c:P * c + P], K("ident"))
                        last.then_inc(x_ht, 1)
                    if t in (3, 4) and valid(k, m, -1):
                        weighted_values(m - 1, k - 1, 1, t - 3)
                    if t == 5 and valid(k, m, 1):
                        maxima_rows(m + 1, k + 1, 0)
                    if k % 2 == 0 and valid(k, m, 4):
                        for w, r in {4: ((0, 0),), 5: ((0, 1),), 6: ((1, 0),), 7: ((1, 1),)}.get(t, ()):
                            project(m, k, w, r)
                    if t == 7 and valid(k, m, 0):
                        weighted_values(m, k, 0, 0)
                    if t == 6 and k % 2 and valid(k, m, 1):
                        n = pair_of(m, k, 1)
                        pe.wait_ge(x_cst, done(n))
                        pe.wait_ge(x_mte, done(2 * (m + 1)))
                        for c in range(2):
                            last = mm(bank[:, 2, P * c:P * c + P], cst[:, P * c:P * c + P], xw[:, 4, :], start=True, stop=True,
                                      skip_group_check=True)
                        last.then_inc(x_v, 1)

            def gate_up(i):
                hf = i % 2
                pe.wait_ge(f_wlo, done(i // 2))
                pe.wait_ge(f_prod, free(i, 2))
                t = slice(512 * hf, 512 * hf + 512)
                for u in range(2):
                    n = 0
                    for c in range(2):
                        for wp, hp in ((0, 0), (0, 1), (1, 0)):
                            last = mm(bank[:, GU[i % 2] + u, :], w_r[:, (i // 2) % WRING, wp, (2 * u + c) * F:(2 * u + c) * F + F],
                                      hT[:, hp, c, t], start=n == 0, stop=n == 5)
                            n += 1
                last.then_inc(f_gu[i % 2], 1)

            def x_first():
                pe.wait_ge(x_consts, 1)
                pe.wait_ge(zeroed, 2)
                pe.wait_ge(a_max, done(NPAIR - 1))

            def residual(tiles):
                for t in tiles:
                    mm(bank[:, ACC[t // 2], D * (t % 2):D * (t % 2) + D], K("ident"), x_sb[:, t, :], start=t % 2 == 0, stop=False,
                       skip_group_check=True)

            def logits(hf):
                n = 0
                for c in range(2):
                    for wp, hp in ((0, 0), (0, 1), (1, 0)):
                        last = mm(bank[:, 5 + hf, :], rw_r[:, wp, c, :], hT[:, hp, c, 512 * hf:512 * hf + 512], start=n == 0, stop=n == 5)
                        n += 1
                last.then_inc(f_lt, 1)

            def down(i):
                e, hf = order(i)
                pe.wait_ge(f_alo, done(i))
                for t in range(4):
                    tt = 4 * hf + t
                    for n, (ap, wp) in enumerate(((0, 0), (0, 1), (1, 0))):
                        last = mm(bank[:, ACC[tt // 2], D * (tt % 2):D * (tt % 2) + D], act_r[:, i % 2, ap, P * t:P * t + P],
                                  w_r[:, (i // 2) % WRING, wp, 4 * F:WE], start=False, stop=(i >= 2 * NE and n == 2), skip_group_check=True)
                    if i >= 2 * NE and t == 1:
                        last.then_inc(f_sum, 1)
                if i >= 2 * NE:
                    last.then_inc(f_sum, 1)
                else:
                    last.then_inc(f_dn, 1)

            def f_first():
                pe.wait_ge(x_hlo, done(3))
                pe.wait_ge(x_max, done(8 * B - 1))
                gate_up(0)
                pe.wait_ge(rw_ready, 1)
                pe.wait_ge(x_exp, done(8 * B - 1))
                logits(0)

            def f_weights():
                pe.wait_ge(x_x2, done(3))
                pe.wait_ge(x_mte, done(2 * B - 1))
                residual(range(2))
                pe.wait_ge(x_n1, done(B - 1))
                residual(range(2, 4))

            all_steps(pe, None, a_step, x_step, x_first, f_weights, f_first, lambda: None)

            pe.wait_ge(x_hlo, done(NPAIR - 1))
            logits(1)
            pe.wait_ge(f_lte, done(1))
            for t in range(NPAIR):
                last = nc.tensor.transpose(bank[:, 0, NE * t:NE * t + NE], lT[:, P * t:P * t + P], K("ident")[0:NE, 0:NE])
            last.then_inc(f_lg, 1)
            down(0)
            gate_up(1)
            gate_up(2)
            pe.wait_ge(f_w, done(0))
            for t in range(NPAIR):
                r = 32 * (t // 4)
                last = mm(bank[r:r + NE, 0, P * (t % 4):P * (t % 4) + P], wsel[:, t, :], K("ident"), start=True, stop=True,
                          skip_group_check=True)
            last.then_inc(f_wtp, 1)
            pe.wait_ge(x_x2, done(NPAIR - 1))
            residual(range(4, 6))
            pe.wait_ge(f_wT, done(0))
            residual(range(6, 8))
            down(1)
            gate_up(3)
            for i in range(2, NI):
                if i == NI - 3:
                    gate_up(NI - 1)
                down(i)
                if i + 2 < NI - 1:
                    gate_up(i + 2)


def kernel(**inp):
    import concourse.bacc as bacc
    from concourse.bass_utils import run_bass_kernel_spmd

    def arr(a):
        return np.ascontiguousarray(np.asarray(a))

    a = {k: arr(v) for k, v in inp.items()}
    partner = np.arange(C) ^ (XD // 2)
    evenodd = np.concatenate([np.arange(HD) + HD * h for h in list(range(0, H, 2)) + list(range(1, H, 2))])
    x2d = a["x"].reshape(NTOK, D)
    chunks = lambda w: w.reshape(2, P, -1).transpose(1, 0, 2)

    def twice(w):
        z = np.zeros((P, P), w.dtype)
        z[:C, :C] = z[C:, C:] = w
        return z

    def spread(w):
        z = np.zeros((P, 2, C), w.dtype)
        for h in range(XH):
            r = XROW * (h % 4)
            z[r:r + XD, h // 4] = w[XD * h:XD * h + XD]
        return z

    qT, kT, vT, oT = (a["L0_xattn_W" + n].T for n in "qkvo")
    bq, bk, bo = (a["L0_xattn_b" + n] for n in "qko")
    gate = np.concatenate([a["L0_ffn_w_gate"], a["L0_ffn_sw_gate"][None]])
    up = np.concatenate([a["L0_ffn_w_up"], a["L0_ffn_sw_up"][None]])
    down = np.concatenate([a["L0_ffn_w_down"], a["L0_ffn_sw_down"][None]])
    A = {
        "x": x2d, "xT": x2d.T, "ctx": a["ctx_2048"].reshape(NTOK, D),
        "wqkv": np.stack([chunks(a["L0_attn_W" + n].T) for n in "qkv"], axis=1),
        "wo": chunks(a["L0_attn_Wo"].T[evenodd]),
        "xw": np.stack([twice(w) for w in (qT, qT[:, partner], kT, kT[:, partner], vT)], axis=1),
        "xwo": spread(oT),
        "xb": np.stack([np.tile(w, 2) for w in (bq, bq[partner], bk, bk[partner], bo)], axis=1),
        "xbv": np.tile(a["L0_xattn_bv"], 4), "rms": a["L0_ffn_rms_weight"],
        "wgu": np.stack([gate, up], axis=1).reshape(NE + 1, 2, 2, P, F).transpose(3, 0, 1, 2, 4),
        "wdn": down.transpose(1, 0, 2),
        "rw": np.concatenate([chunks(a["L0_ffn_router_w"]), np.zeros((P, 2, P - NE), np.float32)], axis=2),
        "con": constant_block()[0], "sel": constant_block()[2],
    }
    nc = bacc.Bacc("TRN2", target_bir_lowering=False, num_devices=1)
    arrays, aps = {}, {}
    for name, v in A.items():
        v = np.ascontiguousarray(v)
        arrays["in_" + name] = v
        aps[name] = nc.dram_tensor("in_" + name, v.shape, mybir.dt.from_np(v.dtype), kind="ExternalInput").ap()
    out = nc.dram_tensor("out_y", (NTOK, D), F32, kind="ExternalOutput").ap()
    build(nc, aps, out)
    r = run_bass_kernel_spmd(nc, [arrays], core_ids=[0])
    return r.results[0]["out_y"].reshape(B, C, D)
```
